# Optimizing a Trainium2 kernel written in Bass

```python
import numpy as np
import jax
import jax.numpy as jnp

def _softmax(x, axis=-1):
    return jax.nn.softmax(x, axis=axis)

def _gelu(x):
    return jax.nn.gelu(x, approximate=True)

def _silu(x):
    return jax.nn.silu(x)

def _sigmoid(x):
    return jax.nn.sigmoid(x)

def _layernorm(x, axis=-1, eps=1e-05):
    m = jnp.mean(x, axis=axis, keepdims=True)
    v = jnp.var(x, axis=axis, keepdims=True)
    return (x - m) / jnp.sqrt(v + eps)

def _scatter_add(tgt, idx, src, axis=0):
    return tgt.at[idx].add(src)

def _segment_sum(src, seg, n):
    return jax.ops.segment_sum(src, seg, n)
kernel_name = 'mk_gnn_ffn_d1_gnn_r32_d017de'

def setup_inputs(seed: int=0):
    np.random.seed(seed)
    _w = jnp.asarray

    def _rec_inputs():
        import jax
        import jax.numpy as jnp
        _gk = jax.random.key(seed)
        x = -0.000125 + 0.9999 * jax.random.normal(jax.random.fold_in(_gk, 1), (2048, 512), jnp.float32)
        src = jax.random.randint(jax.random.fold_in(_gk, 2), (32768,), 0, 2048, jnp.int32)
        dst = jnp.minimum((2048 * jax.random.uniform(jax.random.fold_in(_gk, 3), (32768,)) ** 2.0).astype(jnp.int32), 65535)
        _o = jnp.argsort(dst, stable=True)
        src = src[_o]
        dst = dst[_o]
        edge_weight = jax.random.uniform(jax.random.fold_in(_gk, 12), (32768,), jnp.float32, 0.0, 0.999998)
        return (x, src, dst, edge_weight)
    x, src, dst, edge_weight = _rec_inputs()

    def _L0_gnn_setup():
        import jax, jax.numpy as jnp
        import numpy as np
        N_NODES = 2048
        N_EDGES = 16384
        FEAT_DIM = 512
        EMBED_DIM = 512
        key = jax.random.key(seed)
        k1, k2, k3, k4, k5 = jax.random.split(key, 5)
        x = jax.random.normal(k1, (N_NODES, FEAT_DIM), dtype=jnp.float32)
        limit = float(np.sqrt(6.0 / (EMBED_DIM + FEAT_DIM)))
        weight = jax.random.uniform(k2, (EMBED_DIM, FEAT_DIM), dtype=jnp.float32, minval=-limit, maxval=limit)
        row = jax.random.randint(k3, (N_EDGES,), 0, N_NODES, dtype=jnp.int64)
        col = jax.random.randint(k4, (N_EDGES,), 0, N_NODES, dtype=jnp.int64)
        vals = jax.random.uniform(k5, (N_EDGES,), dtype=jnp.float32)
        return {'x': x, 'weight': weight, 'row': row, 'col': col, 'vals': vals}
    _L0_gnn_all = _L0_gnn_setup()
    _L0_gnn_in = {k: v for k, v in _L0_gnn_all.items() if k in ('weight',)}
    del _L0_gnn_all

    def _L0_ffn_setup():
        import jax, jax.numpy as jnp
        import numpy as np
        D_MODEL, D_FF, N_EXPERTS, TOP_K = (512, 64, 8, 2)
        key = jax.random.key(seed)
        ks = jax.random.split(key, 7)
        B, S = (2, 64)
        x = jax.random.normal(ks[0], (B, S, D_MODEL), dtype=jnp.float32)
        s1 = 1.0 / np.sqrt(D_MODEL)
        s2 = 1.0 / np.sqrt(D_FF)
        Wg = jax.random.normal(ks[1], (D_MODEL, N_EXPERTS), dtype=jnp.float32) * s1
        bg = jnp.zeros((N_EXPERTS,), dtype=jnp.float32)
        W1 = jax.random.normal(ks[2], (N_EXPERTS, D_MODEL, D_FF), dtype=jnp.float32) * s1
        b1 = jax.random.normal(ks[3], (N_EXPERTS, D_FF), dtype=jnp.float32) * s1
        W2 = jax.random.normal(ks[4], (N_EXPERTS, D_FF, D_MODEL), dtype=jnp.float32) * s2
        b2 = jax.random.normal(ks[5], (N_EXPERTS, D_MODEL), dtype=jnp.float32) * s2
        return {'x': x, 'Wg': Wg, 'bg': bg, 'W1': W1, 'b1': b1, 'W2': W2, 'b2': b2}
    _L0_ffn_all = _L0_ffn_setup()
    _L0_ffn_in = {k: v for k, v in _L0_ffn_all.items() if k in ('Wg', 'bg', 'W1', 'b1', 'W2', 'b2')}
    del _L0_ffn_all
    return {'x': x, 'src': src, 'dst': dst, 'edge_weight': edge_weight, 'L0_gnn_weight': _L0_gnn_in['weight'], 'L0_ffn_Wg': _L0_ffn_in['Wg'], 'L0_ffn_bg': _L0_ffn_in['bg'], 'L0_ffn_W1': _L0_ffn_in['W1'], 'L0_ffn_b1': _L0_ffn_in['b1'], 'L0_ffn_W2': _L0_ffn_in['W2'], 'L0_ffn_b2': _L0_ffn_in['b2']}

def reference(x, src, dst, edge_weight, L0_gnn_weight, L0_ffn_Wg, L0_ffn_bg, L0_ffn_W1, L0_ffn_b1, L0_ffn_W2, L0_ffn_b2):
    import jax
    import jax.numpy as jnp

    def _L0_gnn_ref(x, weight, row, col, vals):
        import jax, jax.numpy as jnp
        import numpy as np
        N_NODES = 2048
        N_EDGES = 16384
        FEAT_DIM = 512
        EMBED_DIM = 512
        h = jnp.einsum('nf,ef->ne', x, weight)
        msgs = vals[:, None] * h[col]
        out = jax.ops.segment_sum(msgs, row, num_segments=N_NODES)
        return out

    def _L0_ffn_ref(x, Wg, bg, W1, b1, W2, b2):
        import jax, jax.numpy as jnp
        import numpy as np
        D_MODEL, D_FF, N_EXPERTS, TOP_K = (512, 64, 8, 2)
        B, S, D = x.shape
        xt = x.reshape(B * S, D)
        gate_logits = xt @ Wg + bg
        gate_scores = jax.nn.softmax(gate_logits, axis=-1)
        topk_scores, topk_idx = jax.lax.top_k(gate_scores, TOP_K)
        topk_scores = topk_scores / jnp.sum(topk_scores, axis=-1, keepdims=True)
        combine = jnp.sum(jax.nn.one_hot(topk_idx, N_EXPERTS, dtype=xt.dtype) * topk_scores[..., None], axis=1)
        h = jax.nn.gelu(jnp.einsum('td,edf->etf', xt, W1) + b1[:, None, :], approximate=False)
        expert_out = jnp.einsum('etf,efd->etd', h, W2) + b2[:, None, :]
        out = jnp.einsum('te,etd->td', combine, expert_out)
        return out.reshape(B, S, D)
    x = x + _L0_gnn_ref(_layernorm(x, axis=-1), L0_gnn_weight, src, dst, edge_weight)
    x = x + _L0_ffn_ref(_layernorm(x, axis=-1)[None], L0_ffn_Wg, L0_ffn_bg, L0_ffn_W1, L0_ffn_b1, L0_ffn_W2, L0_ffn_b2)[0]
    return x

_drawn_inputs = setup_inputs


def setup_inputs(seed=0):
    import zlib

    import numpy as np

    out = dict(_drawn_inputs(seed))
    spreads = {'L0_ffn_bg': (0.0, 0.1)}
    factors = {'L0_ffn_b1': 8.0}
    for name, (base, spread) in spreads.items():
        noise = np.random.default_rng([zlib.crc32(name.encode()), seed]).standard_normal(out[name].shape)
        drawn = base * np.exp(spread * noise) if base else spread * noise
        out[name] = jnp.asarray(drawn.astype(out[name].dtype))
    for name, factor in factors.items():
        out[name] = (out[name] * factor).astype(out[name].dtype)
    return out
```

```python
import concourse.bass as bass
from concourse import mybir
from contextlib import ExitStack


F32 = mybir.dt.float32
F16 = mybir.dt.float16
I32 = mybir.dt.int32
U32 = mybir.dt.uint32
ALU = mybir.AluOpType
ACT = mybir.ActivationFunctionType
AX = mybir.AxisListType

P = 128
N, D, E = 2048, 512, 32768
NE, FF = 8, 64
NB = N // P
KD = D // P
KF = NE * FF // P
T = E // P
CH = 2
CT = T // CH
GT = 9
CAP = GT * P
Q = NB * GT
GROUPS = CH * NB
STEP = 8
RB = 4
SUB = 3

SC_W = 4096.0
SC_X = 256.0
SC_M = 256.0
SC_H = 256.0
SC_C = 256.0
EPS = 1e-5
MAGIC = float(0x5F3759DF)


class Order:

    def __init__(self, eng, sem, alone=None):
        self.alone = alone
        self.eng, self.sem, self.done, self.k, self.i, self.per = eng, sem, 0, 0, None, 0

    def loop(self, i, per, times):
        self.i, self.per, self.times, self.k = i, per, times, 0

    def end(self):
        assert self.k == self.per, (self.k, self.per)
        self.done += self.per * self.times
        self.i, self.k = None, 0

    def __call__(self, ins, alone=False):
        ins.then_inc(self.sem, 1)
        self.k += 1
        if self.i is None:
            self.done, self.k = self.done + self.k, 0
            self.eng.wait_ge(self.sem, self.done)
        else:
            wait = self.alone if alone else type(self.eng).wait_ge
            wait(self.eng, self.sem, self.i * self.per + (self.done + self.k))


def gnn_moe(nc, x, src, dst, w, wg, gate_w, gate_b, w1, b1, w2, b2, out, h_dram, cap=CAP):
    ctx = ExitStack()
    with ctx:
        def sb(name, shape, dt):
            return ctx.enter_context(nc.sbuf_tensor(name, shape, dt))

        def sem(name):
            return ctx.enter_context(nc.semaphore(name))

        acc = sb("acc", [P, NB, D], F32)
        src_i = sb("src_i", [P, T], I32)
        dst_i = sb("dst_i", [P, T], I32)
        w_in = sb("w_in", [P, T], F32)
        wg_in = sb("wg_in", [P, KD, D], F32)
        w1_in = sb("w1_in", [P, KD, NE * FF], F32)
        w2_in = sb("w2_in", [P, KF, D], F32)
        gw_in = sb("gw_in", [P, KD, NE], F32)
        b2_in = sb("b2_in", [NE, D], F32)
        gate_bias = sb("gate_bias", [P, NE], F32)
        b1_col = sb("b1_col", [P, KF], F32)
        ident = sb("ident", [P, P], F32)
        tri = sb("tri", [P, P], F16)
        ones = sb("ones", [P, P], F16)
        iota_i = sb("iota_i", [P, Q], I32)
        iota = sb("iota", [P, Q], F16)
        iota8 = sb("iota8", [P, NE], F32)
        expert_rows = sb("expert_rows", [NE, KF, P], F16)
        wgT = sb("wgT", [P, 2, KD, D], F16)
        w1s = sb("w1s", [P, 2, KD, NE * FF], F16)
        w2s = sb("w2s", [P, 2, KF, D], F16)
        gws = sb("gws", [P, 2, KD, NE], F16)
        b2s = sb("b2s", [NE, 2, D], F16)
        block_i = sb("block_i", [P, T], I32)
        local_i = sb("local_i", [P, T], I32)
        block16 = sb("block16", [P, T], F16)
        src_f = sb("src_f", [P, T], F32)
        totals = sb("totals", [P, NB, CH], F32)
        most = sb("most", [P, 1], F32)
        spill_i = sb("spill_i", [P, 1], I32)
        rank = sb("rank", [P, T], F32)
        rank_i = sb("rank_i", [P, T], I32)
        slot_i = sb("slot_i", [P, 2, T], I32)
        slot_f = sb("slot_f", [P, 2, T], F32)
        unfit = sb("unfit", [P, T], F32)
        tmp_t = sb("tmp_t", [P, T], F32)
        w_hi16 = sb("w_hi16", [P, T], F16)
        w_lo16 = sb("w_lo16", [P, T], F16)
        field = sb("field", [P, 4, T], F32)
        rows_oh = sb("rows_oh", [P, 2, STEP, 4, P], F16)
        tile_oh = sb("tile_oh", [P, 2, STEP, Q], F16)
        sorted_f = sb("sorted_f", [P, 4, CH * Q], F32)
        stats = sb("stats", [P, NB, 6], F32)
        mv = sb("mv", [P, NB, 2], F32)
        var = sb("var", [P, NB], F32)
        rstd = sb("rstd", [P, NB], F32)
        newton = sb("newton", [P, NB], F32)
        xn = sb("xn", [P, 2, D], F32)
        xnT = sb("xnT", [P, 2, 2, KD, P], F16)
        rows = sb("rows", [P, 2 * GT, 2 * D], F16)
        words = rows[:, :, :].rearrange("p s d -> p (s d)").bitcast(F32)
        onehot = words[:, 0:2048].bitcast(F16).rearrange("p (b c) -> p b c", b=NB)
        counted = words[:, 2048:4096].rearrange("p (r c) -> p r c", r=2)
        ranked = words[:, 4096:5120]
        rank_part = words[:, 5120:6144].rearrange("p (r c) -> p r c", r=NB // RB)
        keep = words[:, 6144:7168]
        wsel = sb("wsel", [P, 2 * GT, 2, P], F16)
        at_i = sb("at_i", [P, 2, GT], I32)
        at_f = sb("at_f", [P, 2, 3, GT], F32)
        logits = sb("logits", [P, 2, NE], F32)
        top = sb("top", [P, 2, NE], F32)
        top_at = sb("top_at", [P, 2, NE], U32)
        half_top = sb("half_top", [P, 2, 1], F32)
        chosen = sb("chosen", [P, 2, NE], F32)
        th = sb("th", [P, 2, NE], F32)
        den = sb("den", [P, 2, NE], F32)
        share = sb("share", [P, 2, NE], F32)
        share_sum = sb("share_sum", [P, 2, 2], F32)
        shareT = sb("shareT", [NE, 2, 2, P], F16)
        hidden, shared = wg_in[:, 0:2, :], wg_in[:, 2:4, :]
        sharedT = sb("sharedT", [P, 2, 2, KF, P], F16)
        result = sb("result", [P, 2, D], F32)
        spill_at = sb("spill_at", [P, 1], I32)
        spill_rows = sb("spill_rows", [P, 2 * D], F16)
        spill_w = sb("spill_w", [P, 2, T], F32)
        spill_src = sb("spill_src", [P, 1], F32)
        spill_sel = sb("spill_sel", [P, 2, P], F16)

        bank = [ctx.enter_context(nc.psum_tensor(f"bank{i}", [P, D], F32)) for i in range(8)]
        H_BANK, X_BANK = (0, 1), (6, 7)
        SUM_BANK = (0, 1)
        SORT_BANK = (2, 3, 4, 5)
        XT2, UP, SHARE, DOWN, GATE, SHARE_T = 2, 3, 4, 5, 6, 7

        s_src, s_edge, s_wg, s_w1, s_w2, s_small = (sem(n) for n in (
            "src_loaded", "edges_loaded", "wg_loaded", "w1_loaded", "w2_loaded", "small_loaded"))
        s_x = [sem(f"x_loaded{q}") for q in range(4)]
        vec, act, pool = sem("vec_order"), sem("act_order"), sem("pool_order")
        consts_made = sem("consts_made")
        weights_split = sem("weights_split")
        onehot_made, counts_summed, counts_read = sem("onehot_made"), sem("counts_summed"), sem("counts_read")
        wgT_moved, wgT_hi, wgT_split = sem("wgT_moved"), sem("wgT_hi"), sem("wgT_split")
        xn_made, xnT_moved, xnT_hi, xnT_split = sem("xn_made"), sem("xnT_moved"), sem("xnT_hi"), sem("xnT_split")
        h_summed, h_hi, h_split, h_stored = sem("h_summed"), sem("h_hi"), sem("h_split"), sem("h_stored")
        places_made, places_used = sem("places_made"), sem("places_used")
        half_sorted, half_copied = sem("half_sorted"), sem("half_copied")
        staged, wsel_made = sem("staged"), sem("wsel_made")
        gathered = [[sem(f"gathered{h}{k}") for k in range(GT // SUB)] for h in range(2)]
        sums_done, sums_read = sem("sums_done"), sem("sums_read")
        spill_settled = sem("spill_settled")
        sp_idx, sp_got, sp_sel, sp_sum, sp_read = (sem(n) for n in (
            "spill_index", "spill_gathered", "spill_selected", "spill_summed", "spill_added"))
        y_made, yT_moved, yT_hi, yT_split = sem("y_made"), sem("yT_moved"), sem("yT_hi"), sem("yT_split")
        gate_done, top_known, tanh_done, share_made = sem("gate_done"), sem("top_known"), sem("tanh_done"), sem("share_made")
        shareT_moved, shareT_hi, shareT_split = sem("shareT_moved"), sem("shareT_hi"), sem("shareT_split")
        up_done, hidden_made, spread_done = sem("up_done"), sem("hidden_made"), sem("spread_done")
        shared_made, shared_hi, shared_split = sem("shared_made"), sem("shared_hi"), sem("shared_split")
        down_done, result_made = sem("down_done"), sem("result_made")
        stored = [sem(f"stored{h}") for h in range(2)]

        block = ctx.enter_context(nc.Block())

        def wait(eng, semaphore, value):
            if not isinstance(value, int) or value > 0:
                eng.wait_ge(semaphore, value)

        def wait_alone(eng, semaphore, value):
            if not isinstance(value, int):
                value = eng.snap(eng.to_reg(value))
                eng.wait_ge(consts_made, 1)
            eng.wait_ge(semaphore, value)

        def halves(eng, order, per, body, times=NB // 2, first=0):
            with eng.Fori(0, times) as i:
                if order:
                    order.loop(i, per, times)
                for h in range(2):
                    body(i * 2 + (first + h), h)
                if order:
                    order.end()

        @block.sync
        def _(sp):
            sp.dma_start(src_i[:, :], src.rearrange("(p c) -> p c", p=P)).then_inc(s_src, 16)
            sp.dma_start(dst_i[:, :], dst.rearrange("(p c) -> p c", p=P)).then_inc(s_edge, 16)
            sp.dma_start(w_in[:, :], w.rearrange("(p c) -> p c", p=P)).then_inc(s_edge, 16)
            sp.dma_start(wg_in[:, :, :], wg.rearrange("(k p) f -> p k f", p=P)).then_inc(s_wg, 16)
            xv = x.rearrange("(b p) d -> p b d", p=P)
            for q in range(4):
                sp.dma_start(acc[:, 4 * q:4 * q + 4, :], xv[:, 4 * q:4 * q + 4, :]).then_inc(s_x[q], 16)
            for k in range(KD):
                sp.dma_start(w1_in[:, k, :].rearrange("p (e f) -> p e f", e=NE),
                             w1[:, k * P:(k + 1) * P, :].rearrange("e p f -> p e f")).then_inc(s_w1, 16)
            sp.dma_start(w2_in[:, :, :], w2.rearrange("e f d -> (e f) d").rearrange("(k p) d -> p k d", p=P))\
              .then_inc(s_w2, 16)
            sp.dma_start(gw_in[:, :, :], gate_w.rearrange("(k p) e -> p k e", p=P)).then_inc(s_small, 16)
            sp.dma_start(b2_in[:, :], b2).then_inc(s_small, 16)
            sp.dma_start(gate_bias[:, :], gate_b.partition_broadcast(P)).then_inc(s_small, 16)
            sp.dma_start(b1_col[:, :], b1.rearrange("e f -> (e f)").rearrange("(k p) -> p k", p=P),
                         allow_slow_non_contiguous=True).then_inc(s_small, 16)

            with sp.Fori(0, NB) as t:
                sp.wait_ge(h_split, t + 1)
                sp.dma_start(h_dram[bass.ds(t * P, P), :], rows[:, bass.ds(t, 1), :].rearrange("p o d -> p (o d)"))\
                  .then_inc(h_stored, 16)

            def store(b, h):
                sp.wait_ge(result_made, b + 1)
                sp.dma_start(out[bass.ds(b * P, P), :], result[:, h, :]).then_inc(stored[h], 16)
            halves(sp, None, 0, store)
            for h in range(2):
                sp.wait_ge(stored[h], 16 * NB // 2)
            sp.wait_ge(h_stored, 16 * NB)

        @block.gpsimd
        def _(g):
            own = Order(g, pool)
            own(nc.gpsimd.memset(ident[:, :], 0.0))
            own(nc.gpsimd.affine_select(out=ident[:, :], in_=ident[:, :], compare_op=ALU.not_equal, fill=1.0,
                                        base=0, pattern=[[-1, P]], channel_multiplier=1))
            own(nc.gpsimd.memset(tri[:, :], 0.0))
            own(nc.gpsimd.affine_select(out=tri[:, :], in_=tri[:, :], compare_op=ALU.is_gt, fill=-1.0,
                                        base=0, pattern=[[1, P]], channel_multiplier=-1))
            own(nc.gpsimd.memset(ones[:, :], 1.0))
            own(nc.gpsimd.iota(iota_i[:, :], pattern=[[1, Q]], base=0, channel_multiplier=0))
            own(nc.gpsimd.tensor_copy(iota[:, :], iota_i[:, :]))
            own(nc.gpsimd.tensor_copy(iota8[:, :], iota_i[:, 0:NE]))
            own(nc.gpsimd.memset(keep[:, :], 1.0))
            own(nc.gpsimd.memset(keep[:, :].rearrange("p (s c) -> p s c", c=CT)[:, :, 0:1], 0.0))
            own(nc.gpsimd.memset(expert_rows[:, :, :], 0.0))
            own(nc.gpsimd.affine_select(
                out=expert_rows[:, :, :].rearrange("e k (a f) -> e k a f", a=2),
                in_=expert_rows[:, :, :].rearrange("e k (a f) -> e k a f", a=2),
                compare_op=ALU.not_equal, fill=1.0, base=0,
                pattern=[[-2, KF], [-1, 2], [0, FF]], channel_multiplier=1))
            nc.gpsimd.memset(spill_i[:, :], 0).then_inc(consts_made, 1)

            def split(whole, hi, lo):
                own(nc.gpsimd.tensor_scalar(whole, whole, SC_M, None, ALU.mult))
                own(nc.gpsimd.tensor_copy(hi, whole))
                nc.gpsimd.tensor_tensor(lo, whole, hi, ALU.subtract).then_inc(weights_split, 1)

            g.wait_ge(s_w1, 16 * KD)
            split(w1_in[:, :, :], w1s[:, 0, :, :], w1s[:, 1, :, :])
            g.wait_ge(s_w2, 16)
            split(w2_in[:, :, :], w2s[:, 0, :, :], w2s[:, 1, :, :])
            g.wait_ge(s_small, 64)
            split(gw_in[:, :, :], gws[:, 0, :, :], gws[:, 1, :, :])
            split(b2_in[:, :], b2s[:, 0, :], b2s[:, 1, :])

            g.wait_ge(h_stored, 16 * NB)

            def gather(n, h):
                wait_alone(g, staged, n + 1)
                for j in range(GT):
                    g.indirect_dma_start(rows[:, h * GT + j, :], None, h_dram[:, :],
                                         bass.IndirectOffsetOnAxis(ap=at_i[:, h, j:j + 1], axis=0))\
                     .then_inc(gathered[h][j // SUB], 16)
            halves(g, None, 0, gather)

            g.wait_ge(places_made, 2)
            spill = g.value_load(spill_i[0:1, 0:1], min_val=0, max_val=E)
            with g.If(spill > 0):
                with g.Fori(0, T) as t:
                    g.wait_ge(sp_read, t * NB + 1)
                    nc.gpsimd.tensor_copy(spill_at[:, :], dst_i[:, bass.ds(t, 1)]).then_inc(sp_idx, 1)
                    wait_alone(g, sp_idx, t + 1)
                    g.indirect_dma_start(spill_rows[:, :], None, h_dram[:, :],
                                         bass.IndirectOffsetOnAxis(ap=spill_at[:, 0:1], axis=0)).then_inc(sp_got, 16)
            g.wait_ge(spill_settled, 1)
            halves(g, None, 0, lambda n, h: gather(n, h), first=NB)

        @block.scalar
        def _(a):
            own = Order(a, act)
            for k in range(KD):
                a.wait_ge(wgT_moved, k + 1)
                nc.scalar.activation(wgT[:, 0, k, :], bank[4 + k][:, :], ACT.Copy, scale=SC_M).then_inc(wgT_hi, 1)

            def node_tile(t, h):
                a.wait_ge(xnT_moved, t + 1)
                wait(a, h_summed, t)
                nc.scalar.activation(xnT[:, h, 0, :, :].rearrange("p k n -> p (k n)"), bank[X_BANK[h]][:, :],
                                     ACT.Copy, scale=SC_X).then_inc(xnT_hi, 1)
                a.wait_ge(h_summed, t + 1)
                nc.scalar.activation(rows[:, bass.ds(t, 1), 0:D].rearrange("p o d -> p (o d)"), bank[H_BANK[h]][:, :],
                                     ACT.Copy, scale=SC_H / (SC_X * SC_M)).then_inc(h_hi, 1)
            node_tile(0, 0)
            node_tile(1, 1)
            halves(a, None, 0, node_tile, times=NB // 2 - 1, first=2)

            def copy_half(c):
                a.wait_ge(half_sorted, c + 1)
                for f in range(4):
                    nc.scalar.activation(sorted_f[:, f, c * Q:(c + 1) * Q], bank[SORT_BANK[f]][:, 0:Q], ACT.Copy)\
                      .then_inc(half_copied, 1)
                a.wait_ge(half_copied, 4 * (c + 1))

            def stage(n, h, free=True):
                if free:
                    a.wait_ge(sums_done, n - 1)
                nc.scalar.activation(at_f[:, h, :, :], sorted_f[:, 1:4, bass.ds(n * GT, GT)], ACT.Copy)
                nc.scalar.activation(at_i[:, h, :], sorted_f[:, 0, bass.ds(n * GT, GT)], ACT.Copy).then_inc(staged, 1)

            copy_half(0)
            stage(0, 0, free=False)
            stage(1, 1, free=False)
            halves(a, None, 0, lambda n, h: stage(n, h), times=NB // 2 - 1, first=2)
            copy_half(1)

            def rows_hi(b, h):
                a.wait_ge(yT_moved, b + 1)
                nc.scalar.activation(xnT[:, h, 0, :, :].rearrange("p k n -> p (k n)"), bank[XT2][:, :],
                                     ACT.Copy, scale=SC_X).then_inc(yT_hi, 1)

            def gate(b, h):
                a.wait_ge(top_known, b + 1)
                nc.scalar.activation(th[:, h, :], logits[:, h, :], ACT.Tanh, bias=half_top[:, h, :], scale=0.5)\
                  .then_inc(tanh_done, 1)
                a.wait_ge(up_done, b + 1)
                for k in range(KF):
                    last = nc.scalar.activation(hidden[:, h, k * P:(k + 1) * P], bank[UP][:, k * P:(k + 1) * P],
                                                ACT.Gelu, bias=b1_col[:, k:k + 1], scale=1.0 / (SC_X * SC_M))
                last.then_inc(hidden_made, 1)
                a.wait_ge(shareT_moved, b + 1)
                nc.scalar.activation(shareT[:, h, 0, :], bank[SHARE_T][0:NE, 0:P], ACT.Copy, scale=SC_C)\
                  .then_inc(shareT_hi, 1)

            def share_hi(b, h):
                a.wait_ge(shared_made, b + 1)
                nc.scalar.activation(sharedT[:, h, 0, :, :].rearrange("p k n -> p (k n)"), shared[:, h, :],
                                     ACT.Copy).then_inc(shared_hi, 1)

            a.wait_ge(s_small, 64)
            stage(NB, 0)
            stage(NB + 1, 1)
            rows_hi(0, 0)
            gate(0, 0)

            def turn(b, h):
                share_hi(b - 1, 1 - h)
                stage(b + (NB + 1), 1 - h)
                rows_hi(b, h)
                gate(b, h)
            with a.Fori(0, NB // 2 - 1) as i:
                turn(i * 2 + 1, 1)
                turn(i * 2 + 2, 0)
            share_hi(NB - 2, 0)
            rows_hi(NB - 1, 1)
            gate(NB - 1, 1)
            share_hi(NB - 1, 1)

        @block.vector
        def _(v):
            own = Order(v, vec, wait_alone)

            def rsqrt_newton(y, xv, t):
                own(nc.vector.tensor_scalar(xv, xv, EPS, None, ALU.add))
                own(nc.vector.tensor_scalar(y.bitcast(I32), xv.bitcast(I32), -0.5, MAGIC, ALU.mult, ALU.add))
                for _ in range(3):
                    own(nc.vector.tensor_tensor(t, y, y, ALU.mult))
                    own(nc.vector.tensor_tensor(t, t, xv, ALU.mult))
                    own(nc.vector.tensor_scalar(t, t, -0.5, 1.5, ALU.mult, ALU.add))
                    own(nc.vector.tensor_tensor(y, y, t, ALU.mult))

            v.wait_ge(s_src, 16)
            nc.vector.tensor_copy(src_f[:, :], src_i[:, :])
            own(nc.vector.tensor_scalar(block_i[:, :], src_i[:, :], 7, None, ALU.logical_shift_right))
            own(nc.vector.tensor_copy(block16[:, :], block_i[:, :]))
            for b in range(NB):
                last = nc.vector.tensor_scalar(onehot[:, b, :], block16[:, :], float(b), None, ALU.is_equal)
                if b % RB == RB - 1:
                    last.then_inc(onehot_made, 1)
            v.wait_ge(consts_made, 1)
            v.wait_ge(onehot_made, NB // RB)
            for r in range(NB // RB):
                v.wait_ge(counts_summed, r + 1)
                bs = 4 * (r % 2)
                for q in range(2):
                    half = slice(q * D, (q + 1) * D)
                    nc.vector.tensor_tensor_scan(counted[:, r % 2, half], keep[:, half], bank[bs + 2 + q][:, :],
                                                 0.0, ALU.mult, ALU.add)
                    last = None
                own(nc.vector.tensor_copy(
                    tmp_t[:, 0:1], keep[:, 0:1]))
                tiles = counted[:, r % 2, :].rearrange("p (b s c) -> p b s c", b=RB, s=CH)
                nc.vector.tensor_copy(totals[:, r * RB:(r + 1) * RB, :],
                                      tiles[:, :, :, CT - 1:CT].rearrange("p b s o -> p b (s o)"))
                for q in range(2):
                    half = slice(q * D, (q + 1) * D)
                    last = nc.vector.tensor_tensor(ranked[:, half], counted[:, r % 2, half], bank[bs + q][:, :],
                                                   ALU.add)
                last.then_inc(counts_read, 1)
                v.wait_ge(counts_read, r + 1)
                own(nc.vector.tensor_tensor(ranked[:, :], ranked[:, :],
                                            onehot[:, r * RB:(r + 1) * RB, :].rearrange("p b c -> p (b c)"), ALU.mult))
                own(nc.vector.tensor_reduce(rank_part[:, r, :], ranked[:, :].rearrange("p (b c) -> p c b", b=RB),
                                            AX.X, ALU.add))
            nc.vector.tensor_reduce(rank[:, :], rank_part[:, :, :].rearrange("p r c -> p c r"), AX.X, ALU.add)
            own(nc.vector.tensor_reduce(most[:, :], totals[:, :, :].rearrange("p b s -> p (b s)"), AX.X, ALU.max))
            nc.vector.tensor_scalar(spill_i[:, :], most[:, :], -float(cap), 0.0, ALU.add, ALU.max)\
              .then_inc(places_made, 1)
            own(nc.vector.tensor_copy(rank_i[:, :], rank[:, :]))
            nc.vector.tensor_scalar(slot_i[:, 0, :], rank_i[:, :], P - 1, None, ALU.bitwise_and)
            nc.vector.tensor_scalar(slot_i[:, 1, :], rank_i[:, :], 7, None, ALU.logical_shift_right)
            nc.vector.tensor_scalar(local_i[:, :], src_i[:, :], P - 1, None, ALU.bitwise_and)
            own(nc.vector.tensor_scalar(unfit[:, :], rank[:, :], float(cap), None, ALU.is_ge))
            nc.vector.tensor_copy(slot_f[:, :, :], slot_i[:, :, :])
            own(nc.vector.tensor_scalar(tmp_t[:, :], block16[:, :], float(GT), None, ALU.mult))
            own(nc.vector.tensor_tensor(slot_f[:, 1, :], slot_f[:, 1, :], tmp_t[:, :], ALU.add))
            own(nc.vector.scalar_tensor_tensor(slot_f[:, 1, :], unfit[:, :], 4096.0, slot_f[:, 1, :],
                                               ALU.mult, ALU.add))
            v.wait_ge(s_edge, 32)
            nc.vector.tensor_copy(field[:, 0, :], dst_i[:, :])
            nc.vector.tensor_copy(field[:, 1, :], local_i[:, :])
            own(nc.vector.tensor_scalar(w_hi16[:, :], w_in[:, :], SC_W, None, ALU.mult))
            nc.vector.tensor_copy(field[:, 2, :], w_hi16[:, :])
            own(nc.vector.scalar_tensor_tensor(w_lo16[:, :], w_in[:, :], SC_W, w_hi16[:, :],
                                               ALU.mult, ALU.subtract))
            own(nc.vector.tensor_copy(field[:, 3, :], w_lo16[:, :]))
            own(nc.vector.tensor_scalar(tmp_t[:, 0:1], most[:, :], 1.0, None, ALU.mult))

            for k in range(KD):
                v.wait_ge(wgT_hi, k + 1)
                nc.vector.scalar_tensor_tensor(wgT[:, 1, k, :], bank[4 + k][:, :], SC_M, wgT[:, 0, k, :],
                                               ALU.mult, ALU.subtract).then_inc(wgT_split, 1)

            for b in range(NB):
                if b % 4 == 0:
                    v.wait_ge(s_x[b // 4], 16)
                last = nc.vector.bn_stats(stats[:, b, :], acc[:, b, :])
            own(last)
            for b in range(NB):
                last = nc.vector.bn_aggr(mv[:, b, :], stats[:, b, :])
            own(last)
            own(nc.vector.tensor_copy(var[:, :], mv[:, :, 1:2].rearrange("p b o -> p (b o)")))
            rsqrt_newton(rstd[:, :], var[:, :], newton[:, :])

            def node_rows(t, h):
                nc.vector.tensor_scalar(xn[:, h, :], acc[:, bass.ds(t, 1), :].rearrange("p o d -> p (o d)"),
                                        mv[:, bass.ds(t, 1), 0:1].rearrange("p o d -> p (o d)"),
                                        rstd[:, bass.ds(t, 1)], ALU.subtract, ALU.mult).then_inc(xn_made, 1)

            def node_low(t, h):
                v.wait_ge(xnT_hi, t + 1)
                nc.vector.scalar_tensor_tensor(xnT[:, h, 1, :, :].rearrange("p k n -> p (k n)"), bank[X_BANK[h]][:, :],
                                               SC_X, xnT[:, h, 0, :, :].rearrange("p k n -> p (k n)"),
                                               ALU.mult, ALU.subtract).then_inc(xnT_split, 1)
                v.wait_ge(h_hi, t + 1)
                nc.vector.scalar_tensor_tensor(
                    rows[:, bass.ds(t, 1), D:2 * D].rearrange("p o d -> p (o d)"), bank[H_BANK[h]][:, :],
                    SC_H / (SC_X * SC_M), rows[:, bass.ds(t, 1), 0:D].rearrange("p o d -> p (o d)"),
                    ALU.mult, ALU.subtract).then_inc(h_split, 1)

            def node_tile(t, h):
                wait(v, xnT_moved, t)
                node_rows(t, h)
                node_low(t, h)
            node_tile(0, 0)
            node_tile(1, 1)
            halves(v, None, 0, node_tile, times=NB // 2 - 1, first=2)

            def move_step(c, s, h, first=False):
                if not first:
                    v.wait_ge(places_used, c * (CT // STEP) + s - 1)
                for j in range(STEP):
                    at = s * STEP + (c * CT + j)
                    nc.vector.tensor_scalar(tile_oh[:, h, j, :], iota[:, :], slot_f[:, 1, bass.ds(at, 1)], None,
                                            ALU.is_equal)
                    for f in range(4):
                        last = nc.vector.tensor_scalar(rows_oh[:, h, j, f, :], iota[:, 0:P],
                                                       slot_f[:, 0, bass.ds(at, 1)], field[:, f, bass.ds(at, 1)],
                                                       ALU.is_equal, ALU.mult)
                last.then_inc(places_made, 1)
            move_step(0, 0, 0, first=True)
            move_step(0, 1, 1, first=True)
            halves(v, None, 0, lambda s, h: move_step(0, s, h), times=CT // STEP // 2 - 1, first=2)

            def select(n, h):
                v.wait_ge(staged, n + 1)
                for j in range(GT):
                    for half in range(2):
                        last = nc.vector.tensor_scalar(wsel[:, h * GT + j, half, :], iota[:, 0:P],
                                                       at_f[:, h, 0, j:j + 1], at_f[:, h, 1 + half, j:j + 1],
                                                       ALU.is_equal, ALU.mult)
                last.then_inc(wsel_made, 1)

            def add_messages(n, b, h, s, last):
                v.wait_ge(sums_done, n + 1)
                row = acc[:, bass.ds(b, 1), :].rearrange("p o d -> p (o d)")
                ins = nc.vector.scalar_tensor_tensor(row, bank[SUM_BANK[h]][:, :], 1.0 / (SC_W * SC_H), row,
                                                     ALU.mult, ALU.add)
                ins.then_inc(sums_read, 1)

            select(0, 0)

            def first_sweep(n, h, last=False):
                if not last:
                    select(n + 1, 1 - h)
                move_step(1, n, h)
                add_messages(n, n, h, None, None)
            halves(v, None, 0, first_sweep, times=NB // 2 - 1)
            first_sweep(NB - 2, 0)
            first_sweep(NB - 1, 1, last=True)
            v.wait_ge(sums_read, NB)

            spill = v.value_load(spill_i[0:1, 0:1], min_val=0, max_val=E)
            with v.If(spill > 0):
                for half in range(2):
                    nc.vector.tensor_tensor(spill_w[:, half, :], field[:, 2 + half, :], unfit[:, :], ALU.mult)\
                      .then_inc((sp_read, sp_sel)[half], 1)
                v.wait_ge(sp_sel, 1)
                with v.Fori(0, T) as t:
                    nc.vector.tensor_copy(spill_src[:, :], src_f[:, bass.ds(t, 1)]).then_inc(sp_sel, 1)
                    with v.Fori(0, NB) as b:
                        turn = t * NB + b
                        v.wait_ge(sp_sel, turn * 2 + t + 2)
                        for half in range(2):
                            last = nc.vector.tensor_scalar(spill_sel[:, half, :], iota[:, 0:P], spill_src[:, 0:1],
                                                           spill_w[:, half, bass.ds(t, 1)], ALU.is_equal, ALU.mult)
                        last.then_inc(sp_sel, 1)
                        v.wait_ge(sp_sel, turn * 2 + t + 3)
                        nc.vector.tensor_scalar(spill_src[:, :], spill_src[:, :], -float(P), None, ALU.add)\
                          .then_inc(sp_sel, 1)
                        v.wait_ge(sp_sum, turn + 1)
                        row = acc[:, bass.ds(b, 1), :].rearrange("p o d -> p (o d)")
                        nc.vector.scalar_tensor_tensor(row, bank[GATE][:, :], 1.0 / (SC_W * SC_H), row,
                                                       ALU.mult, ALU.add).then_inc(sp_read, 1)
                v.wait_ge(sp_read, T * NB + 1)
            nc.vector.tensor_copy(tmp_t[:, 0:1], most[:, :]).then_inc(spill_settled, 1)

            PER = 29

            def new_rows(b, h):
                add_messages(b + NB, b, h, None, None)
                wait_alone(v, sums_read, b + (NB + 1))
                row = acc[:, bass.ds(b, 1), :].rearrange("p o d -> p (o d)")
                own(nc.vector.bn_stats(stats[:, h, :], row), alone=True)
                own(nc.vector.bn_aggr(mv[:, h, :], stats[:, h, :]))
                rsqrt_newton(rstd[:, h:h + 1], mv[:, h, 1:2], newton[:, h:h + 1])
                nc.vector.tensor_scalar(xn[:, h, :], row, mv[:, h, 0:1], rstd[:, h:h + 1],
                                        ALU.subtract, ALU.mult).then_inc(y_made, 1)

            def experts(b, h):
                v.wait_ge(yT_hi, b + 1)
                nc.vector.scalar_tensor_tensor(xnT[:, h, 1, :, :].rearrange("p k n -> p (k n)"), bank[XT2][:, :],
                                               SC_X, xnT[:, h, 0, :, :].rearrange("p k n -> p (k n)"),
                                               ALU.mult, ALU.subtract).then_inc(yT_split, 1)
                v.wait_ge(gate_done, b + 1)
                own(nc.vector.scalar_tensor_tensor(logits[:, h, :], bank[GATE][:, 0:NE], 1.0 / (SC_X * SC_M),
                                                   gate_bias[:, :], ALU.mult, ALU.add), alone=True)
                own(nc.vector.max(top[:, h, :], logits[:, h, :]))
                nc.vector.tensor_scalar(half_top[:, h, :], top[:, h, 0:1], -0.5, None, ALU.mult)\
                  .then_inc(top_known, 1)
                own(nc.vector.max_index(top_at[:, h, :], top[:, h, :], logits[:, h, :]))
                own(nc.vector.tensor_scalar(chosen[:, h, :], iota8[:, :], top_at[:, h, 0:1], None, ALU.is_equal))
                own(nc.vector.scalar_tensor_tensor(chosen[:, h, :], iota8[:, :], top_at[:, h, 1:2], chosen[:, h, :],
                                                   ALU.is_equal, ALU.add))
                v.wait_ge(tanh_done, b + 1)
                own(nc.vector.tensor_scalar(den[:, h, :], th[:, h, :], -1.0, 1.0, ALU.mult, ALU.add))
                own(nc.vector.reciprocal(den[:, h, :], den[:, h, :]))
                own(nc.vector.scalar_tensor_tensor(share[:, h, :], th[:, h, :], 1.0, den[:, h, :],
                                                   ALU.add, ALU.mult))
                own(nc.vector.tensor_tensor(share[:, h, :], share[:, h, :], chosen[:, h, :], ALU.mult))
                own(nc.vector.tensor_reduce(share_sum[:, h, 0:1], share[:, h, :], AX.X, ALU.add))
                own(nc.vector.reciprocal(share_sum[:, h, 1:2], share_sum[:, h, 0:1]))
                nc.vector.tensor_scalar(share[:, h, :], share[:, h, :], share_sum[:, h, 1:2], None, ALU.mult)\
                  .then_inc(share_made, 1)
                v.wait_ge(shareT_hi, b + 1)
                nc.vector.scalar_tensor_tensor(shareT[:, h, 1, :], bank[SHARE_T][0:NE, 0:P], SC_C, shareT[:, h, 0, :],
                                               ALU.mult, ALU.subtract).then_inc(shareT_split, 1)

            def share_hidden(b, h):
                v.wait_ge(hidden_made, b + 1)
                v.wait_ge(spread_done, b + 1)
                nc.vector.tensor_tensor(shared[:, h, :], hidden[:, h, :], bank[SHARE][:, :], ALU.mult)\
                  .then_inc(shared_made, 1)
                v.wait_ge(shared_hi, b + 1)
                nc.vector.tensor_tensor(sharedT[:, h, 1, :, :].rearrange("p k n -> p (k n)"), shared[:, h, :],
                                        sharedT[:, h, 0, :, :].rearrange("p k n -> p (k n)"), ALU.subtract)\
                  .then_inc(shared_split, 1)

            def finish(b, h, first=False):
                v.wait_ge(down_done, b + 1)
                if not first:
                    v.wait_ge(stored[h], (b - h) * 8)
                row = acc[:, bass.ds(b, 1), :].rearrange("p o d -> p (o d)")
                nc.vector.scalar_tensor_tensor(result[:, h, :], bank[DOWN][:, :], 1.0 / (SC_C * SC_M), row,
                                               ALU.mult, ALU.add).then_inc(result_made, 1)

            select(NB, 0)
            select(NB + 1, 1)
            new_rows(0, 0)
            experts(0, 0)
            halves_per = 2 * (2 + 14 + 12)

            def turn(b, h, first=False, last=False):
                share_hidden(b - 1, 1 - h)
                if not last:
                    select(b + (NB + 1), 1 - h)
                new_rows(b, h)
                experts(b, h)
                finish(b - 1, 1 - h, first=first)

            turn(1, 1, first=True)
            turn(2, 0, first=True)
            with v.Fori(0, NB // 2 - 2) as i:
                own.loop(i, own_per(), NB // 2 - 2)
                turn(i * 2 + 3, 1)
                turn(i * 2 + 4, 0)
                own.end()
            turn(NB - 1, 1, last=True)
            share_hidden(NB - 1, 1)
            finish(NB - 1, 1)

        @block.tensor
        def _(pe):
            def split_product(out_ap, terms):
                n = 0
                for (lh, ll), (rh, rl) in terms:
                    for left, right in ((lh, rh), (lh, rl), (ll, rh)):
                        last = nc.tensor.matmul(out_ap, left, right, start=(n == 0), stop=(n == 3 * len(terms) - 1))
                        n += 1
                return last

            pe.wait_ge(consts_made, 1)
            for r in range(NB // RB):
                pe.wait_ge(onehot_made, r + 1)
                if r >= 2:
                    pe.wait_ge(counts_read, r - 1)
                for q in range(2):
                    oh = onehot[:, r * RB + 2 * q:r * RB + 2 * q + 2, :].rearrange("p b c -> p (b c)")
                    nc.tensor.matmul(bank[4 * (r % 2) + q][:, :], tri[:, :], oh, start=True, stop=True)
                    last = nc.tensor.matmul(bank[4 * (r % 2) + 2 + q][:, :], ones[:, :], oh, start=True, stop=True)
                last.then_inc(counts_summed, 1)
            pe.wait_ge(counts_read, NB // RB)
            pe.wait_ge(s_wg, 16)
            for k in range(KD):
                for e in range(KD):
                    last = nc.tensor.transpose(bank[4 + k][:, e * P:(e + 1) * P], wg_in[:, e, k * P:(k + 1) * P],
                                               ident[:, :])
                last.then_inc(wgT_moved, 1)
            pe.wait_ge(wgT_split, KD)

            def node_tile(t, h):
                pe.wait_ge(xn_made, t + 1)
                wait(pe, xnT_split, t)
                for k in range(KD):
                    last = nc.tensor.transpose(bank[X_BANK[h]][:, k * P:(k + 1) * P], xn[:, h, k * P:(k + 1) * P],
                                               ident[:, :])
                last.then_inc(xnT_moved, 1)
                pe.wait_ge(xnT_split, t + 1)
                wait(pe, h_split, t)
                split_product(bank[H_BANK[h]][:, :],
                              [((xnT[:, h, 0, k, :], xnT[:, h, 1, k, :]), (wgT[:, 0, k, :], wgT[:, 1, k, :]))
                               for k in range(KD)]).then_inc(h_summed, 1)
            node_tile(0, 0)
            node_tile(1, 1)
            halves(pe, None, 0, node_tile, times=NB // 2 - 1, first=2)

            def move_step(c, s, h, start=False, stop=False):
                pe.wait_ge(places_made, c * (CT // STEP) + s + 2)
                for j in range(STEP):
                    for f in range(4):
                        last = nc.tensor.matmul(bank[SORT_BANK[f]][:, 0:Q], rows_oh[:, h, j, f, :], tile_oh[:, h, j, :],
                                                start=start and j == 0, stop=stop and j == STEP - 1)
                last.then_inc(places_used, 1)
                if stop:
                    last = nc.tensor.matmul(bank[7][:, 0:P], ones[:, :], ones[:, :], start=True, stop=True)
                    last.then_inc(half_sorted, 1)

            pe.wait_ge(wgT_split, KD)
            STEPS = CT // STEP
            move_step(0, 0, 0, start=True)
            move_step(0, 1, 1)
            halves(pe, None, 0, lambda s, h: move_step(0, s, h), times=STEPS // 2 - 2, first=2)
            move_step(0, STEPS - 2, 0)
            move_step(0, STEPS - 1, 1, stop=True)

            def messages(n, h, sub, times=None, first=False):
                if sub == 0:
                    pe.wait_ge(wsel_made, n + 1)
                    if not first:
                        pe.wait_ge(sums_read, n - 1)
                pe.wait_ge(gathered[h][sub], (n - h) * (8 * SUB) + 16 * SUB)
                for j in range(sub * SUB, (sub + 1) * SUB):
                    at = h * GT + j
                    for half, cols in ((0, 0), (0, 1), (1, 0)):
                        last = nc.tensor.matmul(bank[SUM_BANK[h]][:, :], wsel[:, at, half, :],
                                                rows[:, at, cols * D:(cols + 1) * D],
                                                start=(j == 0 and half == 0 and cols == 0),
                                                stop=(j == GT - 1 and half == 1))
                if sub == GT // SUB - 1:
                    last.then_inc(sums_done, 1)

            def first_sweep(n, h, first=False, start=False, stop=False):
                if start:
                    pe.wait_ge(half_copied, 4)
                for sub in range(GT // SUB):
                    messages(n, h, sub, first=first)
                move_step(1, n, h, start=start, stop=stop)
            first_sweep(0, 0, first=True, start=True)
            first_sweep(1, 1)
            halves(pe, None, 0, first_sweep, times=NB // 2 - 2, first=2)
            first_sweep(NB - 2, 0)
            first_sweep(NB - 1, 1, stop=True)

            pe.wait_ge(half_copied, 8)
            spill = pe.value_load(spill_i[0:1, 0:1], min_val=0, max_val=E)
            with pe.If(spill > 0):
                with pe.Fori(0, T) as t:
                    wait_alone(pe, sp_got, t * 16 + 16)
                    with pe.Fori(0, NB) as b:
                        turn = t * NB + b
                        pe.wait_ge(sp_sel, turn * 2 + t + 3)
                        pe.wait_ge(sp_read, turn + 1)
                        split_product(bank[GATE][:, :], [((spill_sel[:, 0, :], spill_sel[:, 1, :]),
                                                          (spill_rows[:, 0:D], spill_rows[:, D:2 * D]))])\
                            .then_inc(sp_sum, 1)
            pe.wait_ge(spill_settled, 1)
            pe.wait_ge(weights_split, 4)

            def transpose_rows(b, h):
                pe.wait_ge(y_made, b + 1)
                wait(pe, yT_split, b)
                for k in range(KD):
                    last = nc.tensor.transpose(bank[XT2][:, k * P:(k + 1) * P], xn[:, h, k * P:(k + 1) * P], ident[:, :])
                last.then_inc(yT_moved, 1)

            def gate_and_up(b, h):
                pe.wait_ge(yT_split, b + 1)
                rows_of = [(xnT[:, h, 0, k, :], xnT[:, h, 1, k, :]) for k in range(KD)]
                split_product(bank[GATE][:, 0:NE], [(rows_of[k], (gws[:, 0, k, :], gws[:, 1, k, :]))
                                                    for k in range(KD)]).then_inc(gate_done, 1)
                wait(pe, hidden_made, b)
                for f in range(KF):
                    cols = slice(f * P, (f + 1) * P)
                    last = split_product(bank[UP][:, cols], [((w1s[:, 0, k, cols], w1s[:, 1, k, cols]), rows_of[k])
                                                             for k in range(KD)])
                last.then_inc(up_done, 1)

            def transpose_shares(b, h):
                pe.wait_ge(share_made, b + 1)
                wait(pe, shareT_split, b)
                nc.tensor.transpose(bank[SHARE_T][0:NE, 0:P], share[:, h, :], ident[:, :]).then_inc(shareT_moved, 1)

            def spread_shares(b, h):
                pe.wait_ge(shareT_split, b + 1)
                wait(pe, shared_made, b)
                for k in range(KF):
                    for half in range(2):
                        last = nc.tensor.matmul(bank[SHARE][:, k * P:(k + 1) * P], expert_rows[:, k, :],
                                                shareT[:, h, half, :], start=(half == 0), stop=(half == 1))
                last.then_inc(spread_done, 1)

            def down(b, h):
                pe.wait_ge(shared_split, b + 1)
                wait(pe, result_made, b)
                split_product(bank[DOWN][:, :],
                              [((sharedT[:, h, 0, k, :], sharedT[:, h, 1, k, :]), (w2s[:, 0, k, :], w2s[:, 1, k, :]))
                               for k in range(KF)]
                              + [((shareT[:, h, 0, :], shareT[:, h, 1, :]), (b2s[:, 0, :], b2s[:, 1, :]))])\
                    .then_inc(down_done, 1)

            def second_sweep(b, h, first=False, last=False):
                messages(b + NB, h, 0)
                if not first:
                    transpose_rows(b - 1, 1 - h)
                messages(b + NB, h, 1)
                if not first:
                    gate_and_up(b - 1, 1 - h)
                messages(b + NB, h, 2)
                if not first:
                    transpose_shares(b - 1, 1 - h)
                    spread_shares(b - 1, 1 - h)
                    down(b - 1, 1 - h)

            second_sweep(0, 0, first=True)
            with pe.Fori(0, NB // 2 - 1) as i:
                second_sweep(i * 2 + 1, 1)
                second_sweep(i * 2 + 2, 0)
            second_sweep(NB - 1, 1)
            transpose_rows(NB - 1, 1)
            gate_and_up(NB - 1, 1)
            transpose_shares(NB - 1, 1)
            spread_shares(NB - 1, 1)
            down(NB - 1, 1)


def own_per():
    return 2 * (2 + 14 + 11)


_INS = ['x', 'src', 'dst', 'edge_weight', 'L0_gnn_weight', 'L0_ffn_Wg', 'L0_ffn_bg', 'L0_ffn_W1', 'L0_ffn_b1',
        'L0_ffn_W2', 'L0_ffn_b2']


def kernel(**inputs):
    import numpy as _np
    import concourse.bacc as _bacc
    from concourse import mybir as _mybir
    from concourse.bass_utils import run_bass_kernel_spmd as _run

    nc = _bacc.Bacc("TRN2", target_bir_lowering=False, num_devices=1)
    arrays, args = {}, []
    for name in _INS:
        a = _np.ascontiguousarray(inputs[name])
        arrays[f"in_{name}_dram"] = a
        args.append(nc.dram_tensor(f"in_{name}_dram", a.shape, _mybir.dt.from_np(a.dtype), kind="ExternalInput").ap())
    out = nc.dram_tensor("out_dram", (N, D), _mybir.dt.float32, kind="ExternalOutput").ap()
    h_dram = nc.dram_tensor("h_dram", (N, 2 * D), _mybir.dt.float16, kind="Internal").ap()
    gnn_moe(nc, *args, out, h_dram)
    r = _run(nc, [arrays], core_ids=[0])
    return r.results[0]["out_dram"]
```

```python
import concourse.bass as bass
from concourse import mybir
from contextlib import ExitStack


F32 = mybir.dt.float32
F16 = mybir.dt.float16
I32 = mybir.dt.int32
U32 = mybir.dt.uint32
ALU = mybir.AluOpType
ACT = mybir.ActivationFunctionType
AX = mybir.AxisListType

P = 128
N, D, E = 2048, 512, 32768
NE, FF = 8, 64
NB = N // P
KD = D // P
KF = NE * FF // P
T = E // P
CH = 2
CT = T // CH
GT = 9
CAP = GT * P
Q = NB * GT
GROUPS = CH * NB
STEP = 8
STEPS = CT // STEP
TI = 4
SUB = 3
RB = 4
STACK = 96

SC_W = 4096.0
SC_X = 256.0
SC_M = 256.0
SC_H = 256.0
SC_C = 256.0
EPS = 1e-5
MAGIC = float(0x5F3759DF)


class Order:

    def __init__(self, eng, sem, alone):
        self.eng, self.sem, self.alone = eng, sem, alone
        self.done, self.k, self.i = 0, 0, None

    def loop(self, i, per, times):
        self.i, self.per, self.times, self.k = i, per, times, 0

    def end(self):
        assert self.k == self.per, f"{self.k} completions in a turn"
        self.done += self.per * self.times
        self.i, self.k = None, 0

    def mark(self, ins):
        ins.then_inc(self.sem, 1)
        if self.i is None:
            self.done += 1
            return self.done
        self.k += 1
        return self.i * self.per + (self.done + self.k)

    def __call__(self, ins, alone=False):
        value = self.mark(ins)
        if alone:
            self.alone(self.eng, self.sem, value)
        else:
            self.eng.wait_ge(self.sem, value)


def gnn_moe(nc, x, src, dst, w, wg, gate_w, gate_b, w1, b1, w2, b2, out, h_dram, cap=CAP):
    ctx = ExitStack()
    with ctx:
        def sb(name, shape, dt):
            return ctx.enter_context(nc.sbuf_tensor(name, shape, dt))

        def sem(name):
            return ctx.enter_context(nc.semaphore(name))

        acc = sb("acc", [P, NB, D], F32)
        src_i = sb("src_i", [P, T], I32)
        dst_i = sb("dst_i", [P, T], I32)
        w_in = sb("w_in", [P, T], F32)
        wg_in = sb("wg_in", [P, KD, D], F32)
        w1_in = sb("w1_in", [P, KD, NE * FF], F32)
        w2_in = sb("w2_in", [P, KF, D], F32)
        gw_in = sb("gw_in", [P, KD, NE], F32)
        b2_in = sb("b2_in", [STACK, D], F32)
        gate_bias = sb("gate_bias", [P, NE], F32)
        b1_col = sb("b1_col", [P, KF], F32)
        ident = sb("ident", [P, P], F32)
        ident16 = sb("ident16", [P, P], F16)
        tri = sb("tri", [P, P], F16)
        ones = sb("ones", [P, P], F16)
        iota = sb("iota", [P, P], F16)
        iota_t = sb("iota_t", [P, Q, TI], F16)
        iota_s = sb("iota_s", [P, P, SUB], F16)
        iota8 = sb("iota8", [P, NE], F32)
        expert_rows = sb("expert_rows", [STACK, KF, P], F16)
        wgT = sb("wgT", [P, 2, KD, D], F16)
        w1s = sb("w1s", [P, 2, KD, NE * FF], F16)
        w2s = sb("w2s", [P, 2, KF, D], F16)
        gws = sb("gws", [P, 2, KD, NE], F16)
        b2s = sb("b2s", [STACK, D], F16)
        block_i = sb("block_i", [P, T], I32)
        local_i = sb("local_i", [P, T], I32)
        block16 = sb("block16", [P, T], F16)
        first_tile = sb("first_tile", [P, T], F32)
        spill_i = sb("spill_i", [P, 1], I32)
        rank_i = sb("rank_i", [P, T], I32)
        slot_i = sb("slot_i", [P, 2, T], I32)
        slot = sb("slot", [P, 2, T], F16)
        unfit = sb("unfit", [P, T], F32)
        unfit_sum = sb("unfit_sum", [P, 1], F32)
        unfit16 = sb("unfit16", [P, 1], F16)
        field = sb("field", [P, 4, T], F16)
        w_low = sb("w_low", [P, T], F32)
        plain_oh = sb("plain_oh", [P, 2, STEP // TI, P, TI], F16)
        rows_oh = sb("rows_oh", [P, 2, 4, STEP // TI, P, TI], F16)
        tile_oh = sb("tile_oh", [P, 2, STEP // TI, Q, TI], F16)
        sorted_f = sb("sorted_f", [P, 4, CH * Q], F32)
        sums = sb("sums", [P, NB], F32)
        neg_mean = sb("neg_mean", [P, NB], F32)
        squares = sb("squares", [P, NB], F32)
        shift = sb("shift", [P, NB], F32)
        stats = sb("stats", [P, 4, 6], F32)
        mv = sb("mv", [P, 4, 2], F32)
        var = sb("var", [P, NB], F32)
        rstd = sb("rstd", [P, NB], F32)
        newton = sb("newton", [P, NB], F32)
        xn = sb("xn", [P, 2, D], F32)
        xnT = sb("xnT", [P, 2, 2, KD, P], F16)
        rows = sb("rows", [P, 2 * GT, 2 * D], F16)
        halfwords = rows[:, :, :].rearrange("p s d -> p (s d)")
        onehot = halfwords[:, 0:NB * T].rearrange("p (b c) -> p b c", b=NB)
        counted = halfwords[:, NB * T:2 * NB * T].rearrange("p (b c) -> p b c", b=NB)
        picked = halfwords[:, 2 * NB * T:3 * NB * T].rearrange("p (b c) -> p b c", b=NB)
        keep = halfwords[:, 3 * NB * T:3 * NB * T + RB * T]
        plain_sel = sb("plain_sel", [P, GT // SUB, P, SUB], F16)
        wsel = sb("wsel", [P, 2, 2, GT // SUB, P, SUB], F16)
        at_i = sb("at_i", [P, 2, GT], I32)
        at16 = sb("at16", [P, 2, 3, GT], F16)
        logits = sb("logits", [P, 2, NE], F32)
        top = sb("top", [P, 2, NE], F32)
        top_at = sb("top_at", [P, 2, NE], U32)
        half_top = sb("half_top", [P, 2, 1], F32)
        chosen = sb("chosen", [P, 2, NE], F32)
        th = sb("th", [P, 2, NE], F32)
        den = sb("den", [P, 2, NE], F32)
        share = sb("share", [P, 2, NE], F32)
        share_sum = sb("share_sum", [P, 2, 1], F32)
        share16 = sb("share16", [P, 2, STACK // 32, 32], F16)
        shareT = sb("shareT", [STACK, 2, P], F16)
        hidden, shared = wg_in[:, 0:2, :], wg_in[:, 2:4, :]
        sharedT = sb("sharedT", [P, 2, 2, KF, P], F16)
        result = sb("result", [P, 2, D], F32)
        spill_at = sb("spill_at", [P, 1], I32)
        spill_rows = sb("spill_rows", [P, 2 * D], F16)
        spill_w = sb("spill_w", [P, 2, T], F32)
        spill_src = sb("spill_src", [P, 1], F32)
        spill_sel = sb("spill_sel", [P, 2, P], F16)

        bank = [ctx.enter_context(nc.psum_tensor(f"bank{i}", [P, D], F32)) for i in range(8)]
        H_BANK, X_BANK = (0, 1), (6, 7)
        SUM_BANK = (0, 1)
        SORT_BANK = (2, 3, 4, 5)
        XT2, UP, SHARE, DOWN, GATE, SHARE_T = 2, 3, 4, 5, 6, 7

        s_src, s_edge, s_wg, s_w1, s_w2, s_small = (sem(n) for n in (
            "src_loaded", "edges_loaded", "wg_loaded", "w1_loaded", "w2_loaded", "small_loaded"))
        s_x = [sem(f"x_loaded{q}") for q in range(4)]
        vec, act, pool = sem("vec_order"), sem("act_order"), sem("pool_order")
        consts_made, weights_split = sem("consts_made"), sem("weights_split")
        onehot_made, counts_summed, picked_made = sem("onehot_made"), sem("counts_summed"), sem("picked_made")
        ranks_summed, unfit_made, unfit_summed, spill_known = (
            sem("ranks_summed"), sem("unfit_made"), sem("unfit_summed"), sem("spill_known"))
        w_low_made = sem("w_low_made")
        wgT_moved, wgT_hi, wgT_split = sem("wgT_moved"), sem("wgT_hi"), sem("wgT_split")
        squares_made, rstd_made = sem("squares_made"), sem("rstd_made")
        xn_made, xnT_moved, xnT_hi, xnT_split = sem("xn_made"), sem("xnT_moved"), sem("xnT_hi"), sem("xnT_split")
        h_summed, h_hi, h_split, h_stored = sem("h_summed"), sem("h_hi"), sem("h_split"), sem("h_stored")
        plain_made, low_made, places_made, places_used = (
            sem("plain_made"), sem("low_made"), sem("places_made"), sem("places_used"))
        half_sorted, half_copied = sem("half_sorted"), sem("half_copied")
        staged, wsel_made = sem("staged"), sem("wsel_made")
        gathered = [[sem(f"gathered{h}{k}") for k in range(GT // SUB)] for h in range(2)]
        sums_done, sums_read = sem("sums_done"), sem("sums_read")
        sp_idx, sp_got, sp_sel, sp_sum, sp_read = (sem(n) for n in (
            "spill_index", "spill_gathered", "spill_selected", "spill_summed", "spill_added"))
        y_made, yT_moved, yT_hi, yT_split = sem("y_made"), sem("yT_moved"), sem("yT_hi"), sem("yT_split")
        gate_done, top_known, tanh_done, share_made = sem("gate_done"), sem("top_known"), sem("tanh_done"), sem("share_made")
        shareT_moved, shareT_made = sem("shareT_moved"), sem("shareT_made")
        up_done, hidden_made, spread_done = sem("up_done"), sem("hidden_made"), sem("spread_done")
        shared_made, shared_hi, shared_split = sem("shared_made"), sem("shared_hi"), sem("shared_split")
        down_done, result_made = sem("down_done"), sem("result_made")
        stored = [sem(f"stored{h}") for h in range(2)]

        block = ctx.enter_context(nc.Block())

        def wait(eng, semaphore, value):
            if not isinstance(value, int) or value > 0:
                eng.wait_ge(semaphore, value)

        def wait_alone(eng, semaphore, value):
            if not isinstance(value, int):
                value = eng.snap(eng.to_reg(value))
                eng.wait_ge(consts_made, 1)
            eng.wait_ge(semaphore, value)

        def sweep(eng, body, start, loop, stop, order=None, per=0):
            a, b = loop
            for n in range(start, a):
                body(n, n % 2)
            with eng.Fori(0, (b - a) // 2) as i:
                if order:
                    order.loop(i, per, (b - a) // 2)
                body(i * 2 + a, a % 2)
                body(i * 2 + (a + 1), (a + 1) % 2)
                if order:
                    order.end()
            for n in range(b, stop):
                body(n, n % 2)

        def known(n, low, high):
            return not isinstance(n, int) or low <= n < high

        NODES = (0, (2, NB - 2), NB)
        FIRST = (0, (2, NB - 4), NB)
        SECOND = (0, (4, NB - 2), NB + 3)

        @block.sync
        def _(sp):
            sp.dma_start(src_i[:, :], src.rearrange("(p c) -> p c", p=P)).then_inc(s_src, 16)
            xv = x.rearrange("(b p) d -> p b d", p=P)
            for q in range(4):
                sp.dma_start(acc[:, 4 * q:4 * q + 4, :], xv[:, 4 * q:4 * q + 4, :]).then_inc(s_x[q], 16)
                if q == 0:
                    sp.dma_start(wg_in[:, :, :], wg.rearrange("(k p) f -> p k f", p=P)).then_inc(s_wg, 16)
                    sp.dma_start(dst_i[:, :], dst.rearrange("(p c) -> p c", p=P)).then_inc(s_edge, 16)
                    sp.dma_start(w_in[:, :], w.rearrange("(p c) -> p c", p=P)).then_inc(s_edge, 16)
            for k in range(KD):
                sp.dma_start(w1_in[:, k, :].rearrange("p (e f) -> p e f", e=NE),
                             w1[:, k * P:(k + 1) * P, :].rearrange("e p f -> p e f")).then_inc(s_w1, 16)
            sp.dma_start(w2_in[:, :, :], w2.rearrange("e f d -> (e f) d").rearrange("(k p) d -> p k d", p=P))\
              .then_inc(s_w2, 16)
            sp.dma_start(gw_in[:, :, :], gate_w.rearrange("(k p) e -> p k e", p=P)).then_inc(s_small, 16)
            sp.dma_start(gate_bias[:, :], gate_b.partition_broadcast(P)).then_inc(s_small, 16)
            sp.dma_start(b1_col[:, :], b1.rearrange("e f -> (e f)").rearrange("(k p) -> p k", p=P),
                         allow_slow_non_contiguous=True).then_inc(s_small, 16)
            sp.wait_ge(consts_made, 1)
            for row in range(0, STACK, 32):
                sp.dma_start(b2_in[row:row + NE, :], b2).then_inc(s_small, 16)

            with sp.Fori(0, NB) as t:
                sp.wait_ge(h_split, t + 1)
                sp.dma_start(h_dram[bass.ds(t * P, P), :], rows[:, bass.ds(t, 1), :].rearrange("p o d -> p (o d)"))\
                  .then_inc(h_stored, 16)

            def store(b, h):
                sp.wait_ge(result_made, b + 1)
                sp.dma_start(out[bass.ds(b * P, P), :], result[:, h, :]).then_inc(stored[h], 16)
            sweep(sp, store, 0, (0, NB), NB)
            for h in range(2):
                sp.wait_ge(stored[h], 16 * NB // 2)
            sp.wait_ge(h_stored, 16 * NB)

        @block.gpsimd
        def _(g):
            own = Order(g, pool, wait_alone)
            own(nc.gpsimd.memset(tri[:, :], 0.0))
            own(nc.gpsimd.affine_select(out=tri[:, :], in_=tri[:, :], compare_op=ALU.is_gt, fill=-1.0,
                                        base=0, pattern=[[1, P]], channel_multiplier=-1))
            own(nc.gpsimd.memset(ones[:, :], 1.0))
            own(nc.gpsimd.memset(keep, 1.0))
            own(nc.gpsimd.memset(keep.rearrange("p (s c) -> p s c", c=CT)[:, :, 0:1], 0.0))
            for eye in (ident, ident16):
                own(nc.gpsimd.memset(eye[:, :], 0.0))
                own(nc.gpsimd.affine_select(out=eye[:, :], in_=eye[:, :], compare_op=ALU.not_equal, fill=1.0,
                                            base=0, pattern=[[-1, P]], channel_multiplier=1))
            own(nc.gpsimd.memset(b2_in[:, :], 0.0))
            nc.gpsimd.memset(share16[:, :, :, :], 0.0).then_inc(consts_made, 1)
            own(nc.gpsimd.iota(iota[:, :], pattern=[[1, P]], base=0, channel_multiplier=0,
                               allow_small_or_imprecise_dtypes=True))
            own(nc.gpsimd.iota(iota_t[:, :, :], pattern=[[1, Q], [0, TI]], base=0, channel_multiplier=0,
                               allow_small_or_imprecise_dtypes=True))
            own(nc.gpsimd.iota(iota_s[:, :, :], pattern=[[1, P], [0, SUB]], base=0, channel_multiplier=0,
                               allow_small_or_imprecise_dtypes=True))
            own(nc.gpsimd.iota(iota8[:, :], pattern=[[1, NE]], base=0, channel_multiplier=0,
                               allow_small_or_imprecise_dtypes=True))
            own(nc.gpsimd.memset(expert_rows[:, :, :], 0.0))
            for row in (0, 64):
                part = expert_rows[row:row + NE, :, :].rearrange("e k (a f) -> e k a f", a=2)
                last = nc.gpsimd.affine_select(out=part, in_=part, compare_op=ALU.not_equal, fill=1.0, base=0,
                                               pattern=[[-2, KF], [-1, 2], [0, FF]], channel_multiplier=1)
                own(last)
            nc.gpsimd.memset(spill_at[:, :], 0).then_inc(consts_made, 1)

            def scaled(whole, hi):
                own(nc.gpsimd.tensor_scalar(whole, whole, SC_M, None, ALU.mult))
                own(nc.gpsimd.tensor_copy(hi, whole))

            def split(n, whole, hi, lo):
                scaled(whole, hi)
                nc.gpsimd.tensor_tensor(lo, whole, hi, ALU.subtract).then_inc(weights_split, 1)
                g.wait_ge(weights_split, n)

            g.wait_ge(s_w1, 16 * KD)
            split(1, w1_in[:, :, :], w1s[:, 0, :, :], w1s[:, 1, :, :])
            g.wait_ge(s_w2, 16)
            split(2, w2_in[:, :, :], w2s[:, 0, :, :], w2s[:, 1, :, :])
            g.wait_ge(s_small, 96)
            split(3, gw_in[:, :, :], gws[:, 0, :, :], gws[:, 1, :, :])
            scaled(b2_in[:, :], b2s[:, :])
            low = slice(32, 32 + NE)
            nc.gpsimd.tensor_tensor(b2s[low, :], b2_in[low, :], b2s[low, :], ALU.subtract).then_inc(weights_split, 1)
            g.wait_ge(weights_split, 4)

            g.wait_ge(h_stored, 16 * NB)

            def gather(n, h):
                wait_alone(g, staged, n + 1)
                for j in range(GT):
                    g.indirect_dma_start(rows[:, h * GT + j, :], None, h_dram[:, :],
                                         bass.IndirectOffsetOnAxis(ap=at_i[:, h, j:j + 1], axis=0))\
                     .then_inc(gathered[h][j // SUB], 16)
            sweep(g, gather, 0, (0, NB), NB)

            g.wait_ge(spill_known, 1)
            spill = g.value_load(spill_i[0:1, 0:1], min_val=0, max_val=E)
            with g.If(spill > 0):
                with g.Fori(0, T) as t:
                    g.wait_ge(sp_read, t * NB + 1)
                    nc.gpsimd.tensor_copy(spill_at[:, :], dst_i[:, bass.ds(t, 1)]).then_inc(sp_idx, 1)
                    wait_alone(g, sp_idx, t + 1)
                    g.indirect_dma_start(spill_rows[:, :], None, h_dram[:, :],
                                         bass.IndirectOffsetOnAxis(ap=spill_at[:, 0:1], axis=0)).then_inc(sp_got, 16)
            sweep(g, gather, NB, (NB, 2 * NB), 2 * NB)

        @block.scalar
        def _(a):
            own = Order(a, act, wait_alone)
            for q in range(3):
                a.wait_ge(s_x[q], 16)
                tiles = range(4 * q, 4 * q + 4)
                for b in tiles:
                    last = nc.scalar.activation(xn[:, b % 2, :], acc[:, b, :], ACT.Copy, accum_out=sums[:, b:b + 1])
                    own(last)
                four = slice(4 * q, 4 * q + 4)
                own(nc.scalar.activation(neg_mean[:, four], sums[:, four], ACT.Copy, scale=-1.0 / D))
                for b in tiles:
                    own(nc.scalar.activation(xn[:, b % 2, :], acc[:, b, :], ACT.Square, bias=neg_mean[:, b:b + 1],
                                             accum_out=squares[:, b:b + 1]))
            nc.scalar.activation(sums[:, 0:1], neg_mean[:, 0:1], ACT.Copy).then_inc(squares_made, 1)
            for k in range(KD):
                a.wait_ge(wgT_moved, k + 1)
                nc.scalar.activation(wgT[:, 0, k, :], bank[4 + k][:, :], ACT.Copy, scale=SC_M).then_inc(wgT_hi, 1)
            a.wait_ge(unfit_summed, 1)
            nc.scalar.activation(spill_i[:, :], bank[1][:, 0:1], ACT.Copy).then_inc(spill_known, 1)
            a.wait_ge(rstd_made, 1)

            def rows_of(t, h):
                wait(a, xnT_moved, t - 1)
                nc.scalar.activation(xn[:, h, :], acc[:, bass.ds(t, 1), :].rearrange("p o d -> p (o d)"),
                                     ACT.Identity, bias=shift[:, bass.ds(t, 1)], scale=rstd[:, bass.ds(t, 1)])\
                  .then_inc(xn_made, 1)

            def transposed_hi(t, h):
                a.wait_ge(xnT_moved, t + 1)
                wait(a, h_summed, t - 1)
                nc.scalar.activation(xnT[:, h, 0, :, :].rearrange("p k n -> p (k n)"), bank[X_BANK[h]][:, :],
                                     ACT.Copy, scale=SC_X).then_inc(xnT_hi, 1)

            def places_low(c, s, h):
                a.wait_ge(plain_made, s + (c * STEPS + 1))
                for j in range(STEP):
                    last = nc.scalar.activation(rows_oh[:, h, 3, j // TI, :, j % TI], plain_oh[:, h, j // TI, :, j % TI],
                                                ACT.Copy, scale=w_low[:, bass.ds(s * STEP + (c * CT + j), 1)])
                last.then_inc(low_made, 1)

            def node(t, h):
                if known(t, 0, NB - 1):
                    transposed_hi(t + 1, 1 - h)
                if known(t, 0, NB - 2):
                    rows_of(t + 2, h)
                if known(t, 0, NB - 1):
                    places_low(0, t + 1, 1 - h)
                a.wait_ge(h_summed, t + 1)
                nc.scalar.activation(rows[:, bass.ds(t, 1), 0:D].rearrange("p o d -> p (o d)"), bank[H_BANK[h]][:, :],
                                     ACT.Copy, scale=SC_H / (SC_X * SC_M)).then_inc(h_hi, 1)
            rows_of(0, 0)
            rows_of(1, 1)
            transposed_hi(0, 0)
            places_low(0, 0, 0)
            sweep(a, node, *NODES)

            def copy_half(c):
                a.wait_ge(half_sorted, c + 1)
                for f in range(4):
                    nc.scalar.activation(sorted_f[:, f, c * Q:(c + 1) * Q], bank[SORT_BANK[f]][:, 0:Q], ACT.Copy)\
                      .then_inc(half_copied, 1)
                a.wait_ge(half_copied, 4 * (c + 1))

            def stage(n, h):
                wait(a, sums_done, n - 1)
                nc.scalar.activation(at16[:, h, :, :], sorted_f[:, 1:4, bass.ds(n * GT, GT)], ACT.Copy)
                nc.scalar.activation(at_i[:, h, :], sorted_f[:, 0, bass.ds(n * GT, GT)], ACT.Copy).then_inc(staged, 1)

            copy_half(0)
            stage(0, 0)
            stage(1, 1)

            def first_sweep(n, h):
                if isinstance(n, int) and n == 0:
                    places_low(1, 2, 0)
                    places_low(1, 3, 1)
                elif known(n, 1, NB - 3):
                    places_low(1, n + 3, 1 - h)
                elif n == NB - 2:
                    copy_half(1)
                stage(n + 2, h)
            places_low(1, 0, 0)
            places_low(1, 1, 1)
            sweep(a, first_sweep, *FIRST)

            a.wait_ge(s_small, 96)

            def second_sweep(p, h):
                if known(p, 2, NB + 2):
                    b, bh = p - 2, h
                    a.wait_ge(shared_made, b + 1)
                    nc.scalar.activation(sharedT[:, bh, 0, :, :].rearrange("p k n -> p (k n)"), shared[:, bh, :],
                                         ACT.Copy).then_inc(shared_hi, 1)
                if known(p, 1, NB + 1):
                    b, bh = p - 1, 1 - h
                    a.wait_ge(yT_moved, b + 1)
                    nc.scalar.activation(xnT[:, bh, 0, :, :].rearrange("p k n -> p (k n)"), bank[XT2][:, :],
                                         ACT.Copy, scale=SC_X).then_inc(yT_hi, 1)
                    a.wait_ge(top_known, b + 1)
                    nc.scalar.activation(th[:, bh, :], logits[:, bh, :], ACT.Tanh, bias=half_top[:, bh, :], scale=0.5)\
                      .then_inc(tanh_done, 1)
                    a.wait_ge(up_done, b + 1)
                    for k in range(KF):
                        last = nc.scalar.activation(hidden[:, bh, k * P:(k + 1) * P], bank[UP][:, k * P:(k + 1) * P],
                                                    ACT.Gelu, bias=b1_col[:, k:k + 1], scale=1.0 / (SC_X * SC_M))
                    last.then_inc(hidden_made, 1)
                    a.wait_ge(shareT_moved, b + 1)
                    nc.scalar.activation(shareT[:, bh, :], bank[SHARE_T][0:STACK, 0:P // 2].bitcast(F16), ACT.Copy)\
                      .then_inc(shareT_made, 1)
                if known(p, 0, NB - 2):
                    stage(p + (NB + 2), h)
            sweep(a, second_sweep, *SECOND)

        @block.vector
        def _(v):
            own = Order(v, vec, wait_alone)

            def rsqrt_newton(y, xv, t):
                nc.vector.tensor_scalar(y.bitcast(I32), xv.bitcast(I32), -0.5, MAGIC, ALU.mult, ALU.add)
                own(nc.vector.tensor_scalar(xv, xv, -0.5, None, ALU.mult))
                for _ in range(3):
                    if y.shape[-1] == 1:
                        own(nc.vector.scalar_tensor_tensor(t, y, y, xv, ALU.mult, ALU.mult))
                    else:
                        own(nc.vector.tensor_tensor(t, y, y, ALU.mult))
                        own(nc.vector.tensor_tensor(t, t, xv, ALU.mult))
                    own(nc.vector.scalar_tensor_tensor(y, t, 1.5, y, ALU.add, ALU.mult))

            v.wait_ge(s_src, 16)
            own(nc.vector.tensor_scalar(block_i[:, :], src_i[:, :], 7, None, ALU.logical_shift_right))
            own(nc.vector.tensor_copy(block16[:, :], block_i[:, :]))
            v.wait_ge(consts_made, 1)
            for b in range(NB):
                last = nc.vector.tensor_scalar(onehot[:, b, :], block16[:, :], float(b), None, ALU.is_equal)
            own(last)
            for r in range(NB // RB):
                some = slice(r * RB, (r + 1) * RB)
                nc.vector.tensor_tensor_scan(counted[:, some, :].rearrange("p b c -> p (b c)"), keep,
                                             onehot[:, some, :].rearrange("p b c -> p (b c)"),
                                             0.0, ALU.mult, ALU.add).then_inc(onehot_made, 1)
            nc.vector.tensor_scalar(local_i[:, :], src_i[:, :], P - 1, None, ALU.bitwise_and)
            own(nc.vector.tensor_scalar(first_tile[:, :], block16[:, :], float(GT), None, ALU.mult))
            v.wait_ge(s_edge, 32)
            nc.vector.tensor_copy(field[:, 1, :], local_i[:, :])
            nc.vector.tensor_copy(field[:, 0, :], dst_i[:, :])
            own(nc.vector.tensor_scalar(field[:, 2, :], w_in[:, :], SC_W, None, ALU.mult))
            own(nc.vector.scalar_tensor_tensor(field[:, 3, :], w_in[:, :], SC_W, field[:, 2, :],
                                               ALU.mult, ALU.subtract))
            nc.vector.tensor_copy(w_low[:, :], field[:, 3, :]).then_inc(w_low_made, 1)
            for r in range(NB // RB):
                v.wait_ge(counts_summed, r + 1)
                for q in range(2):
                    two = slice(r * RB + 2 * q, r * RB + 2 * q + 2)
                    last = nc.vector.scalar_tensor_tensor(
                        picked[:, two, :].rearrange("p b c -> p (b c)"), bank[2 * r + q][:, :], 2047.0,
                        onehot[:, two, :].rearrange("p b c -> p (b c)"), ALU.min, ALU.mult)
                last.then_inc(picked_made, 1)
            v.wait_ge(ranks_summed, 1)
            rank = bank[0][:, 0:T]
            nc.vector.tensor_scalar(unfit[:, :], rank, float(cap), 0.0, ALU.is_ge, ALU.add, accum_out=unfit_sum[:, :])
            own(nc.vector.tensor_copy(rank_i[:, :], rank))
            own(nc.vector.tensor_scalar(slot_i[:, 1, :], rank_i[:, :], 7, None, ALU.logical_shift_right))
            nc.vector.tensor_copy(unfit16[:, :], unfit_sum[:, :]).then_inc(unfit_made, 1)
            own(nc.vector.tensor_scalar(slot_i[:, 0, :], rank_i[:, :], P - 1, None, ALU.bitwise_and))
            own(nc.vector.tensor_tensor(first_tile[:, :], first_tile[:, :], slot_i[:, 1, :], ALU.add))
            nc.vector.tensor_copy(slot[:, 0, :], slot_i[:, 0, :])
            own(nc.vector.scalar_tensor_tensor(slot[:, 1, :], unfit[:, :], 4096.0, first_tile[:, :],
                                               ALU.mult, ALU.add))

            v.wait_ge(s_x[3], 16)
            done = 3 * NB // 4
            for b in range(done, NB):
                last = nc.vector.bn_stats(stats[:, b - done, :], acc[:, b, :])
            own(last)
            for b in range(done, NB):
                last = nc.vector.bn_aggr(mv[:, b - done, :], stats[:, b - done, :])
            own(last)
            nc.vector.tensor_scalar(neg_mean[:, done:], mv[:, :, 0], -1.0, None, ALU.mult)
            nc.vector.tensor_scalar(var[:, done:], mv[:, :, 1], EPS, None, ALU.add)
            v.wait_ge(squares_made, 1)
            own(nc.vector.tensor_scalar(var[:, :done], squares[:, :done], 1.0 / D, EPS, ALU.mult, ALU.add))
            rsqrt_newton(rstd[:, :], var[:, :], newton[:, :])
            nc.vector.tensor_tensor(shift[:, :], neg_mean[:, :], rstd[:, :], ALU.mult).then_inc(rstd_made, 1)
            for k in range(KD):
                v.wait_ge(wgT_hi, k + 1)
                nc.vector.scalar_tensor_tensor(wgT[:, 1, k, :], bank[4 + k][:, :], SC_M, wgT[:, 0, k, :],
                                               ALU.mult, ALU.subtract).then_inc(wgT_split, 1)
            v.wait_ge(consts_made, 2)

            def transposed_low(t, h):
                v.wait_ge(xnT_hi, t + 1)
                nc.vector.scalar_tensor_tensor(xnT[:, h, 1, :, :].rearrange("p k n -> p (k n)"), bank[X_BANK[h]][:, :],
                                               SC_X, xnT[:, h, 0, :, :].rearrange("p k n -> p (k n)"),
                                               ALU.mult, ALU.subtract).then_inc(xnT_split, 1)

            def h_low(t, h):
                v.wait_ge(h_hi, t + 1)
                nc.vector.scalar_tensor_tensor(
                    rows[:, bass.ds(t, 1), D:2 * D].rearrange("p o d -> p (o d)"), bank[H_BANK[h]][:, :],
                    SC_H / (SC_X * SC_M), rows[:, bass.ds(t, 1), 0:D].rearrange("p o d -> p (o d)"),
                    ALU.mult, ALU.subtract).then_inc(h_split, 1)

            def spread(tiles, groups, ti, width):
                return tiles.rearrange("p (g t) -> p g t", t=ti).unsqueeze(2).to_broadcast([P, groups, width, ti])

            def repeated(table, groups, width, ti):
                return table[:, 0:width, :].unsqueeze(1).to_broadcast([P, groups, width, ti])

            def places_plain(c, s, h):
                if not isinstance(s, int) or c * STEPS + s >= 2:
                    v.wait_ge(places_used, s + (c * STEPS - 1))
                G = STEP // TI
                at = bass.ds(s * STEP + c * CT, STEP)
                nc.vector.tensor_tensor(plain_oh[:, h], repeated(iota_t, G, P, TI), spread(slot[:, 0, at], G, TI, P),
                                        ALU.is_equal).then_inc(plain_made, 1)

            def places(c, s, h):
                G = STEP // TI
                at = bass.ds(s * STEP + c * CT, STEP)
                nc.vector.tensor_tensor(tile_oh[:, h], repeated(iota_t, G, Q, TI), spread(slot[:, 1, at], G, TI, Q),
                                        ALU.is_equal)
                v.wait_ge(plain_made, s + (c * STEPS + 1))
                for f in range(3):
                    last = nc.vector.tensor_tensor(rows_oh[:, h, f], plain_oh[:, h], spread(field[:, f, at], G, TI, P),
                                                   ALU.mult)
                last.then_inc(places_made, 1)

            def node(t, h):
                if known(t, 0, NB - 1):
                    places_plain(0, t + 1, 1 - h)
                    transposed_low(t + 1, 1 - h)
                if known(t, 1, NB):
                    h_low(t - 1, 1 - h)
                if known(t, 0, NB - 1):
                    places(0, t + 1, 1 - h)
            places_plain(0, 0, 0)
            places(0, 0, 0)
            transposed_low(0, 0)
            sweep(v, node, *NODES)
            h_low(NB - 1, 1)

            def select(n, h):
                v.wait_ge(staged, n + 1)
                wait(v, wsel_made, n)
                G = GT // SUB
                own(nc.vector.tensor_tensor(plain_sel[:, :, :, :], repeated(iota_s, G, P, SUB),
                                            spread(at16[:, h, 0, :], G, SUB, P), ALU.is_equal))
                for half in range(2):
                    last = nc.vector.tensor_tensor(wsel[:, h, half], plain_sel[:, :, :, :],
                                                   spread(at16[:, h, 1 + half, :], G, SUB, P), ALU.mult)
                last.then_inc(wsel_made, 1)

            def add_messages(n, b, h):
                v.wait_ge(sums_done, n + 1)
                row = acc[:, bass.ds(b, 1), :].rearrange("p o d -> p (o d)")
                nc.vector.scalar_tensor_tensor(row, bank[SUM_BANK[h]][:, :], 1.0 / (SC_W * SC_H), row,
                                               ALU.mult, ALU.add).then_inc(sums_read, 1)

            def places_all(s, h):
                places_plain(1, s, h)
                places(1, s, h)
            places_all(0, 0)
            places_all(1, 1)
            select(0, 0)

            def first_sweep(n, h):
                select(n + 1, 1 - h)
                if isinstance(n, int) and n == 0:
                    places_all(2, 0)
                    places_all(3, 1)
                elif known(n, 1, NB - 3):
                    places_all(n + 3, 1 - h)
                add_messages(n, n, h)
            sweep(v, first_sweep, *FIRST, order=own, per=2)
            v.wait_ge(sums_read, NB)

            v.wait_ge(spill_known, 1)
            spill = v.value_load(spill_i[0:1, 0:1], min_val=0, max_val=E)
            with v.If(spill > 0):
                for half in range(2):
                    nc.vector.tensor_tensor(spill_w[:, half, :], field[:, 2 + half, :], unfit[:, :], ALU.mult)\
                      .then_inc((sp_read, sp_sel)[half], 1)
                with v.Fori(0, T) as t:
                    v.wait_ge(sp_sel, t * (2 * NB + 1) + 1)
                    nc.vector.tensor_copy(spill_src[:, :], src_i[:, bass.ds(t, 1)]).then_inc(sp_sel, 1)
                    with v.Fori(0, NB) as b:
                        turn = t * NB + b
                        v.wait_ge(sp_sel, turn * 2 + t + 2)
                        for half in range(2):
                            last = nc.vector.tensor_scalar(spill_sel[:, half, :], iota[:, :], spill_src[:, 0:1],
                                                           spill_w[:, half, bass.ds(t, 1)], ALU.is_equal, ALU.mult)
                        last.then_inc(sp_sel, 1)
                        v.wait_ge(sp_sel, turn * 2 + t + 3)
                        nc.vector.tensor_scalar(spill_src[:, :], spill_src[:, :], -float(P), None, ALU.add)\
                          .then_inc(sp_sel, 1)
                        v.wait_ge(sp_sum, turn + 1)
                        row = acc[:, bass.ds(b, 1), :].rearrange("p o d -> p (o d)")
                        nc.vector.scalar_tensor_tensor(row, bank[GATE][:, :], 1.0 / (SC_W * SC_H), row,
                                                       ALU.mult, ALU.add).then_inc(sp_read, 1)
                v.wait_ge(sp_read, T * NB + 1)

            def new_rows(b, h):
                add_messages(b + NB, b, h)
                wait_alone(v, sums_read, b + (NB + 1))
                row = acc[:, bass.ds(b, 1), :].rearrange("p o d -> p (o d)")
                own(nc.vector.bn_stats(stats[:, h, :], row), alone=True)
                own(nc.vector.bn_aggr(mv[:, h, :], stats[:, h, :]))
                own(nc.vector.tensor_scalar(var[:, h:h + 1], mv[:, h, 1:2], EPS, None, ALU.add))
                rsqrt_newton(rstd[:, h:h + 1], var[:, h:h + 1], newton[:, h:h + 1])
                nc.vector.tensor_scalar(xn[:, h, :], row, mv[:, h, 0:1], rstd[:, h:h + 1],
                                        ALU.subtract, ALU.mult).then_inc(y_made, 1)

            def shares(b, h):
                v.wait_ge(yT_hi, b + 1)
                nc.vector.scalar_tensor_tensor(xnT[:, h, 1, :, :].rearrange("p k n -> p (k n)"), bank[XT2][:, :],
                                               SC_X, xnT[:, h, 0, :, :].rearrange("p k n -> p (k n)"),
                                               ALU.mult, ALU.subtract).then_inc(yT_split, 1)
                v.wait_ge(gate_done, b + 1)
                own(nc.vector.scalar_tensor_tensor(logits[:, h, :], bank[GATE][:, 0:NE], 1.0 / (SC_X * SC_M),
                                                   gate_bias[:, :], ALU.mult, ALU.add), alone=True)
                own(nc.vector.max(top[:, h, :], logits[:, h, :]))
                nc.vector.tensor_scalar(half_top[:, h, :], top[:, h, 0:1], -0.5, None, ALU.mult)\
                  .then_inc(top_known, 1)
                own(nc.vector.max_index(top_at[:, h, :], top[:, h, :], logits[:, h, :]))
                own(nc.vector.tensor_scalar(chosen[:, h, :], iota8[:, :], top_at[:, h, 0:1], None, ALU.is_equal))
                own(nc.vector.scalar_tensor_tensor(chosen[:, h, :], iota8[:, :], top_at[:, h, 1:2], chosen[:, h, :],
                                                   ALU.is_equal, ALU.add))
                v.wait_ge(tanh_done, b + 1)
                own(nc.vector.tensor_scalar(den[:, h, :], th[:, h, :], -1.0, 1.0, ALU.mult, ALU.add))
                own(nc.vector.reciprocal(den[:, h, :], den[:, h, :]))
                own(nc.vector.scalar_tensor_tensor(share[:, h, :], th[:, h, :], 1.0, den[:, h, :],
                                                   ALU.add, ALU.mult))
                own(nc.vector.scalar_tensor_tensor(share[:, h, :], share[:, h, :], 1.0, chosen[:, h, :],
                                                   ALU.mult, ALU.mult, accum_out=share_sum[:, h, :]))
                own(nc.vector.reciprocal(share_sum[:, h, :], share_sum[:, h, :]))
                own(nc.vector.tensor_scalar(share[:, h, :], share[:, h, :], share_sum[:, h, :], SC_C,
                                            ALU.mult, ALU.mult))
                own(nc.vector.tensor_copy(share16[:, h, 0:2, 0:NE],
                                          share[:, h, :].unsqueeze(1).to_broadcast([P, 2, NE])))
                nc.vector.tensor_tensor(share16[:, h, 2, 0:NE], share[:, h, :], share16[:, h, 0, 0:NE], ALU.subtract)\
                  .then_inc(share_made, 1)

            def second_sweep(p, h):
                if known(p, 2, NB + 2):
                    b, bh = p - 2, h
                    v.wait_ge(hidden_made, b + 1)
                    v.wait_ge(spread_done, b + 1)
                    nc.vector.tensor_tensor(shared[:, bh, :], hidden[:, bh, :], bank[SHARE][:, :], ALU.mult)\
                      .then_inc(shared_made, 1)
                if known(p, 3, NB + 3):
                    b, bh = p - 3, 1 - h
                    v.wait_ge(down_done, b + 1)
                    if not isinstance(b, int) or b >= 2:
                        v.wait_ge(stored[bh], (b - bh) * 8)
                    row = acc[:, bass.ds(b, 1), :].rearrange("p o d -> p (o d)")
                    nc.vector.scalar_tensor_tensor(result[:, bh, :], bank[DOWN][:, :], 1.0 / (SC_C * SC_M), row,
                                                   ALU.mult, ALU.add).then_inc(result_made, 1)
                if known(p, 2, NB + 2):
                    b, bh = p - 2, h
                    v.wait_ge(shared_hi, b + 1)
                    nc.vector.tensor_tensor(sharedT[:, bh, 1, :, :].rearrange("p k n -> p (k n)"), shared[:, bh, :],
                                            sharedT[:, bh, 0, :, :].rearrange("p k n -> p (k n)"), ALU.subtract)\
                      .then_inc(shared_split, 1)
                if known(p, 1, NB + 1):
                    shares(p - 1, 1 - h)
                if known(p, 0, NB - 1):
                    select(p + (NB + 1), 1 - h)
                if known(p, 0, NB):
                    new_rows(p, h)
            sweep(v, second_sweep, *SECOND, order=own, per=2 * (12 + 1 + 10))

        @block.tensor
        def _(pe):
            def split_product(out_ap, pairs, more=()):
                terms = [t for (lh, ll), (rh, rl) in pairs for t in ((lh, rh), (lh, rl), (ll, rh))] + list(more)
                for n, (left, right) in enumerate(terms):
                    last = nc.tensor.matmul(out_ap, left, right, start=(n == 0), stop=(n == len(terms) - 1))
                return last

            pe.wait_ge(consts_made, 1)
            for r in range(NB // RB):
                pe.wait_ge(onehot_made, r + 1)
                for q in range(2):
                    two = slice(r * RB + 2 * q, r * RB + 2 * q + 2)
                    nc.tensor.matmul(bank[2 * r + q][:, :], ones[:, :],
                                     counted[:, two, :].rearrange("p b c -> p (b c)"), start=True, stop=False)
                    last = nc.tensor.matmul(bank[2 * r + q][:, :], tri[:, :],
                                            onehot[:, two, :].rearrange("p b c -> p (b c)"), start=False, stop=True)
                last.then_inc(counts_summed, 1)
            for r in range(NB // RB):
                pe.wait_ge(picked_made, r + 1)
                for b in range(r * RB, (r + 1) * RB):
                    last = nc.tensor.matmul(bank[0][:, 0:T], ident16[:, :], picked[:, b, :],
                                            start=(b == 0), stop=(b == NB - 1))
            last.then_inc(ranks_summed, 1)
            pe.wait_ge(s_wg, 16)
            for k in range(KD):
                for e in range(KD):
                    last = nc.tensor.transpose(bank[4 + k][:, e * P:(e + 1) * P], wg_in[:, e, k * P:(k + 1) * P],
                                               ident[:, :])
                last.then_inc(wgT_moved, 1)
            pe.wait_ge(unfit_made, 1)
            nc.tensor.matmul(bank[1][:, 0:1], ones[:, :], unfit16[:, :], start=True, stop=True)\
                .then_inc(unfit_summed, 1)
            pe.wait_ge(wgT_split, KD)

            def transpose_node(t, h):
                pe.wait_ge(xn_made, t + 1)
                wait(pe, xnT_split, t - 1)
                for k in range(KD):
                    last = nc.tensor.transpose(bank[X_BANK[h]][:, k * P:(k + 1) * P], xn[:, h, k * P:(k + 1) * P],
                                               ident[:, :])
                last.then_inc(xnT_moved, 1)

            def move(c, s, h, start=False, stop=False):
                pe.wait_ge(places_made, s + (c * STEPS + 1))
                pe.wait_ge(low_made, s + (c * STEPS + 1))
                for j in range(STEP):
                    for f in range(4):
                        last = nc.tensor.matmul(bank[SORT_BANK[f]][:, 0:Q], rows_oh[:, h, f, j // TI, :, j % TI],
                                                tile_oh[:, h, j // TI, :, j % TI],
                                                start=start and j == 0, stop=stop and j == STEP - 1)
                last.then_inc(places_used, 1)
                if stop:
                    nc.tensor.matmul(bank[7][:, 0:P], ones[:, :], ones[:, :], start=True, stop=True)\
                        .then_inc(half_sorted, 1)

            def node(t, h):
                if known(t, 0, NB - 1):
                    transpose_node(t + 1, 1 - h)
                pe.wait_ge(xnT_split, t + 1)
                wait(pe, h_split, t - 1)
                split_product(bank[H_BANK[h]][:, :],
                              [((xnT[:, h, 0, k, :], xnT[:, h, 1, k, :]), (wgT[:, 0, k, :], wgT[:, 1, k, :]))
                               for k in range(KD)]).then_inc(h_summed, 1)
                if isinstance(t, int) and t == NB - 1:
                    pe.wait_ge(xnT_split, NB)
                move(0, t, h, start=isinstance(t, int) and t == 0, stop=isinstance(t, int) and t == STEPS - 1)
            transpose_node(0, 0)
            sweep(pe, node, *NODES)

            def messages(n, h, sub):
                if sub == 0:
                    pe.wait_ge(wsel_made, n + 1)
                    if not isinstance(n, int) or n >= 2:
                        pe.wait_ge(sums_read, n - 1)
                pe.wait_ge(gathered[h][sub], (n - h) * (8 * SUB) + 16 * SUB)
                for t in range(SUB):
                    for half, cols in ((0, 0), (0, 1), (1, 0)):
                        last = nc.tensor.matmul(bank[SUM_BANK[h]][:, :], wsel[:, h, half, sub, :, t],
                                                rows[:, h * GT + sub * SUB + t, cols * D:(cols + 1) * D],
                                                start=(sub == 0 and t == 0 and half == 0 and cols == 0),
                                                stop=(sub == GT // SUB - 1 and t == SUB - 1 and half == 1))
                if sub == GT // SUB - 1:
                    last.then_inc(sums_done, 1)

            pe.wait_ge(half_copied, 4)
            pe.wait_ge(h_split, NB)

            def first_sweep(n, h):
                if isinstance(n, int) and n < 2:
                    move(1, 2 * n, 0, start=(n == 0))
                    messages(n, h, 0)
                    move(1, 2 * n + 1, 1)
                    messages(n, h, 1)
                    messages(n, h, 2)
                    return
                messages(n, h, 0)
                messages(n, h, 1)
                if known(n, 2, NB - 2):
                    move(1, n + 2, h, stop=isinstance(n, int) and n == NB - 3)
                messages(n, h, 2)
            sweep(pe, first_sweep, *FIRST)

            pe.wait_ge(half_copied, 8)
            pe.wait_ge(spill_known, 1)
            spill = pe.value_load(spill_i[0:1, 0:1], min_val=0, max_val=E)
            with pe.If(spill > 0):
                with pe.Fori(0, T) as t:
                    wait_alone(pe, sp_got, t * 16 + 16)
                    with pe.Fori(0, NB) as b:
                        turn = t * NB + b
                        pe.wait_ge(sp_sel, turn * 2 + t + 3)
                        pe.wait_ge(sp_read, turn + 1)
                        split_product(bank[GATE][:, :], [((spill_sel[:, 0, :], spill_sel[:, 1, :]),
                                                          (spill_rows[:, 0:D], spill_rows[:, D:2 * D]))])\
                            .then_inc(sp_sum, 1)
            pe.wait_ge(weights_split, 4)

            def second_sweep(p, h):
                b, bh = p - 1, 1 - h
                if known(p, 0, NB):
                    messages(p + NB, h, 0)
                if known(p, 1, NB + 1):
                    pe.wait_ge(y_made, b + 1)
                    wait(pe, yT_split, b)
                    for k in range(KD):
                        last = nc.tensor.transpose(bank[XT2][:, k * P:(k + 1) * P], xn[:, bh, k * P:(k + 1) * P],
                                                   ident[:, :])
                    last.then_inc(yT_moved, 1)
                if known(p, 0, NB):
                    messages(p + NB, h, 1)
                if known(p, 1, NB + 1):
                    pe.wait_ge(yT_split, b + 1)
                    halves_of = [(xnT[:, bh, 0, k, :], xnT[:, bh, 1, k, :]) for k in range(KD)]
                    split_product(bank[GATE][:, 0:NE], [(halves_of[k], (gws[:, 0, k, :], gws[:, 1, k, :]))
                                                        for k in range(KD)]).then_inc(gate_done, 1)
                    wait(pe, hidden_made, b)
                    for f in range(KF):
                        cols = slice(f * P, (f + 1) * P)
                        last = split_product(bank[UP][:, cols], [((w1s[:, 0, k, cols], w1s[:, 1, k, cols]), halves_of[k])
                                                                 for k in range(KD)])
                    last.then_inc(up_done, 1)
                if known(p, 0, NB):
                    messages(p + NB, h, 2)
                if known(p, 1, NB + 1):
                    pe.wait_ge(share_made, b + 1)
                    wait(pe, shareT_made, b)
                    nc.tensor.transpose(bank[SHARE_T][0:STACK, 0:P // 2].bitcast(F16),
                                        share16[:, bh].rearrange("p s e -> p (s e)"), ident16[:, :])\
                        .then_inc(shareT_moved, 1)
                if known(p, 2, NB + 2):
                    d, dh = p - 2, h
                    pe.wait_ge(shared_split, d + 1)
                    wait(pe, result_made, d)
                    split_product(bank[DOWN][:, :],
                                  [((sharedT[:, dh, 0, k, :], sharedT[:, dh, 1, k, :]),
                                    (w2s[:, 0, k, :], w2s[:, 1, k, :])) for k in range(KF)],
                                  more=[(shareT[:, dh, :], b2s[:, :])]).then_inc(down_done, 1)
                if known(p, 1, NB + 1):
                    pe.wait_ge(shareT_made, b + 1)
                    wait(pe, shared_made, b)
                    for k in range(KF):
                        last = nc.tensor.matmul(bank[SHARE][:, k * P:(k + 1) * P], expert_rows[:, k, :],
                                                shareT[:, bh, :], start=True, stop=True)
                    last.then_inc(spread_done, 1)
            sweep(pe, second_sweep, *SECOND)


_INS = ['x', 'src', 'dst', 'edge_weight', 'L0_gnn_weight', 'L0_ffn_Wg', 'L0_ffn_bg', 'L0_ffn_W1', 'L0_ffn_b1',
        'L0_ffn_W2', 'L0_ffn_b2']


def kernel(**inputs):
    import numpy as _np
    import concourse.bacc as _bacc
    from concourse import mybir as _mybir
    from concourse.bass_utils import run_bass_kernel_spmd as _run

    nc = _bacc.Bacc("TRN2", target_bir_lowering=False, num_devices=1)
    arrays, args = {}, []
    for name in _INS:
        a = _np.ascontiguousarray(inputs[name])
        arrays[f"in_{name}_dram"] = a
        args.append(nc.dram_tensor(f"in_{name}_dram", a.shape, _mybir.dt.from_np(a.dtype), kind="ExternalInput").ap())
    out = nc.dram_tensor("out_dram", (N, D), _mybir.dt.float32, kind="ExternalOutput").ap()
    h_dram = nc.dram_tensor("h_dram", (N, 2 * D), _mybir.dt.float16, kind="Internal").ap()
    gnn_moe(nc, *args, out, h_dram)
    r = _run(nc, [arrays], core_ids=[0])
    return r.results[0]["out_dram"]
```

```python
import concourse.bass as bass
from concourse import mybir
from contextlib import ExitStack


F32 = mybir.dt.float32
F16 = mybir.dt.float16
I32 = mybir.dt.int32
U32 = mybir.dt.uint32
ALU = mybir.AluOpType
ACT = mybir.ActivationFunctionType

P = 128
N, D, E = 2048, 512, 32768
NE, FF = 8, 64
NB = N // P
KD = D // P
KF = NE * FF // P
T = E // P
PIECES = ((0, 2), (2, 4), (4, 8), (8, 12), (12, 14), (14, 16))
RB = 4
PARTS = 2
CT = (T * 3 // 8, T * 5 // 8)
C0 = (0, CT[0])
GT = (7, 11)
GTM = max(GT)
CAP = tuple(g * P for g in GT)
Q = tuple(NB * g for g in GT)
Q0 = (0, Q[0])
QM = max(Q)
STEP = 8
STEPS = tuple(c // STEP for c in CT)
S0 = (0, STEPS[0])
TI = 4
SUB = tuple(tuple(min(TI, g - t) for t in range(0, g, TI)) for g in GT)
SUBS = tuple(len(n) for n in SUB)
SLOTS = 2 * GTM
SLOT0 = ((GTM - GT[0], GTM), (0, GTM))
OUTER = GTM - GT[0]
INNER = 2 * GT[0]
FOLDED = 2
assert FOLDED * TI == 2 * KD and all(n == TI for n in SUB[1][:FOLDED])
assert OUTER * 2 * D == 4 * STEP * P and 3 * NB * T + RB * T <= INNER * 2 * D
STACK = 96

SC_W = 4096.0
SC_X = 256.0
SC_M = 256.0
SC_H = 256.0
SC_C = 256.0
EPS = 1e-5
MAGIC = float(0x5F3759DF)


class Order:

    def __init__(self, eng, sem, alone):
        self.eng, self.sem, self.alone = eng, sem, alone
        self.done, self.k, self.i = 0, 0, None

    def loop(self, i, per, times):
        self.i, self.per, self.times, self.k = i, per, times, 0

    def end(self):
        assert self.k == self.per, f"{self.k} completions in a turn"
        self.done += self.per * self.times
        self.i, self.k = None, 0

    def mark(self, ins):
        ins.then_inc(self.sem, 1)
        if self.i is None:
            self.done += 1
            return self.done
        self.k += 1
        return self.i * self.per + (self.done + self.k)

    def __call__(self, ins, alone=False):
        value = self.mark(ins)
        if alone:
            self.alone(self.eng, self.sem, value)
        else:
            self.eng.wait_ge(self.sem, value)


def gnn_moe(nc, x, src, dst, w, wg, gate_w, gate_b, w1, b1, w2, b2, out, h_dram, cap=CAP):
    ctx = ExitStack()
    with ctx:
        def sb(name, shape, dt):
            return ctx.enter_context(nc.sbuf_tensor(name, shape, dt))

        def sem(name):
            return ctx.enter_context(nc.semaphore(name))

        acc = sb("acc", [P, NB, D], F32)
        src_i = sb("src_i", [P, T], I32)
        dst_i = sb("dst_i", [P, T], I32)
        w_in = sb("w_in", [P, T], F32)
        wg_in = sb("wg_in", [P, KD, D], F32)
        w1_in = sb("w1_in", [P, KD, NE * FF], F32)
        w2_in = sb("w2_in", [P, KF, D], F32)
        gw_in = sb("gw_in", [P, KD, NE], F32)
        b2_in = sb("b2_in", [STACK, D], F32)
        gate_bias = sb("gate_bias", [P, NE], F32)
        b1_col = sb("b1_col", [P, KF], F32)
        ident = sb("ident", [P, P], F32)
        ident16 = sb("ident16", [P, P], F16)
        tri = sb("tri", [P, P], F16)
        ones = sb("ones", [P, P], F16)
        iota = sb("iota", [P, P], F16)
        iota_t = sb("iota_t", [P, QM, TI], F16)
        iota8 = sb("iota8", [P, NE], F32)
        expert_rows = sb("expert_rows", [STACK, KF, P], F16)
        wgT = sb("wgT", [P, 2, KD, D], F16)
        ratio_rows = wgT
        w1s = sb("w1s", [P, 2, KD, NE * FF], F16)
        w2s = sb("w2s", [P, 2, KF, D], F16)
        gws = sb("gws", [P, 2, KD, NE], F16)
        b2s = sb("b2s", [STACK, D], F16)
        block_i = sb("block_i", [P, T], I32)
        local_i = sb("local_i", [P, T], I32)
        block16 = sb("block16", [P, T], F16)
        first_tile = sb("first_tile", [P, T], F32)
        spill_i = sb("spill_i", [P, 1], I32)
        rank_i = sb("rank_i", [P, T], I32)
        slot_i = sb("slot_i", [P, 2, T], I32)
        slot = sb("slot", [P, 2, T], F16)
        unfit = sb("unfit", [P, T], F32)
        unfit_sum = sb("unfit_sum", [P, PARTS], F32)
        unfit16 = sb("unfit16", [P, 1], F16)
        field = sb("field", [P, 4, T], F16)
        w_low = sb("w_low", [P, T], F32)
        plain_oh = sb("plain_oh", [P, 2, STEP // TI, P, TI], F16)
        tile_oh = sb("tile_oh", [P, 2, STEP // TI, QM, TI], F16)
        sorted_f = sb("sorted_f", [P, 4, sum(Q)], F32)
        sums = sb("sums", [P, NB], F32)
        neg_mean = sb("neg_mean", [P, NB], F32)
        squares = sb("squares", [P, NB], F32)
        shift = sb("shift", [P, NB], F32)
        stats = sb("stats", [P, 2, 6], F32)
        mv = sb("mv", [P, 2, 2], F32)
        var = sb("var", [P, NB], F32)
        rstd = sb("rstd", [P, NB], F32)
        newton = sb("newton", [P, NB], F32)
        xn = sb("xn", [P, 2, D], F32)
        xnT = sb("xnT", [P, 2, 2, KD, P], F16)
        rows = sb("rows", [P, SLOTS, 2 * D], F16)
        result = sb("result", [P, 2, D], F32)
        rows_oh = [rows[:, a:a + OUTER, :].rearrange("p s d -> p (s d)")
                   .rearrange("p (f g r t) -> p f g r t", f=4, g=STEP // TI, r=P) for a in (0, SLOTS - OUTER)]
        halfwords = rows[:, OUTER:SLOTS - OUTER, :].rearrange("p s d -> p (s d)")
        onehot = halfwords[:, 0:NB * T].rearrange("p (b c) -> p b c", b=NB)
        counted = halfwords[:, NB * T:2 * NB * T].rearrange("p (b c) -> p b c", b=NB)
        picked = halfwords[:, 2 * NB * T:3 * NB * T].rearrange("p (b c) -> p b c", b=NB)
        keep = halfwords[:, 3 * NB * T:3 * NB * T + RB * T]
        plain_sel = sb("plain_sel", [P, max(SUBS), P, TI], F16)
        wsel = sb("wsel", [P, 2, 2, max(SUBS), P, TI], F16)
        ratio = sb("ratio", [P, Q[1]], F32)
        ratio_den = sb("ratio_den", [P, Q[1]], F32)
        at_i = sb("at_i", [P, 2, GTM], I32)
        at16 = sb("at16", [P, 2, 3, max(SUBS) * TI], F16)
        logits = sb("logits", [P, 2, NE], F32)
        top = sb("top", [P, 2, NE], F32)
        top_at = sb("top_at", [P, 2, NE], U32)
        top_f = sb("top_f", [P, 2, 2], F32)
        lead = sb("lead", [P, 2, 1], F32)
        tanh_half = sb("tanh_half", [P, 2, 1], F32)
        top_share = sb("top_share", [P, 2, 2], F32)
        second_share = sb("second_share", [P, 2, NE], F32)
        share = sb("share", [P, 2, NE], F32)
        share16 = sb("share16", [P, 2, STACK // 32, 32], F16)
        shareT = sb("shareT", [STACK, 2, P], F16)
        hidden, shared = wg_in[:, 0:2, :], wg_in[:, 2:4, :]
        sharedT = sb("sharedT", [P, 2, 2, KF, P], F16)
        spill_at = sb("spill_at", [P, 1], I32)
        spill_rows = sb("spill_rows", [P, 2 * D], F16)
        spill_w = sb("spill_w", [P, 2, T], F32)
        spill_src = sb("spill_src", [P, 1], F32)
        spill_sel = sb("spill_sel", [P, 2, P], F16)

        bank = [ctx.enter_context(nc.psum_tensor(f"bank{i}", [P, D], F32)) for i in range(8)]
        H_BANK, X_BANK = (0, 1), (6, 7)
        SUM_BANK = (0, 1)
        SORT_BANK = (2, 3, 4, 5)
        XT2, UP, SHARE, DOWN, GATE, SHARE_T = 2, 3, 4, 5, 6, 7

        s_src, s_edge, s_wg, s_w1, s_w2, s_small = (sem(n) for n in (
            "src_loaded", "edges_loaded", "wg_loaded", "w1_loaded", "w2_loaded", "small_loaded"))
        s_x = [sem(f"x_loaded{q}") for q in range(len(PIECES))]
        vec, act, pool = sem("vec_order"), sem("act_order"), sem("pool_order")
        consts_made, weights_split = sem("consts_made"), sem("weights_split")
        onehot_made, counts_summed, picked_made = sem("onehot_made"), sem("counts_summed"), sem("picked_made")
        ranks_summed, unfit_made, unfit_summed, spill_known = (
            sem("ranks_summed"), sem("unfit_made"), sem("unfit_summed"), sem("spill_known"))
        w_low_made = sem("w_low_made")
        wgT_moved, wgT_hi, wgT_split = sem("wgT_moved"), sem("wgT_hi"), sem("wgT_split")
        squares_made, rstd_made = sem("squares_made"), sem("rstd_made")
        xn_made, xnT_moved, xnT_hi, xnT_split = sem("xn_made"), sem("xnT_moved"), sem("xnT_hi"), sem("xnT_split")
        h_summed, h_hi, h_split, h_stored = sem("h_summed"), sem("h_hi"), sem("h_split"), sem("h_stored")
        plain_made, low_made, places_made, places_used = (
            sem("plain_made"), sem("low_made"), sem("places_made"), sem("places_used"))
        part_sorted, part_copied = sem("part_sorted"), sem("part_copied")
        ratio_made, ratio_rows_made, folded = sem("ratio_made"), sem("ratio_rows_made"), sem("folded")
        sel_made, high_made = sem("sel_made"), sem("high_made")
        staged, wsel_made = sem("staged"), sem("wsel_made")
        gathered = [[sem(f"gathered{h}{k}") for k in range(max(SUBS))] for h in range(2)]
        sums_done, sums_read = sem("sums_done"), sem("sums_read")
        sp_idx, sp_got, sp_sel, sp_sum, sp_read = (sem(n) for n in (
            "spill_index", "spill_gathered", "spill_selected", "spill_summed", "spill_added"))
        mean_known, squares2_made, shift_known = sem("mean_known"), sem("squares2_made"), sem("shift_known")
        y_made, yT_moved, yT_hi, yT_split = sem("y_made"), sem("yT_moved"), sem("yT_hi"), sem("yT_split")
        gate_done, top_known, tanh_done, share_made = sem("gate_done"), sem("top_known"), sem("tanh_done"), sem("share_made")
        shareT_moved, shareT_made = sem("shareT_moved"), sem("shareT_made")
        up_done, hidden_made, spread_done = sem("up_done"), sem("hidden_made"), sem("spread_done")
        shared_made, shared_hi, shared_split = sem("shared_made"), sem("shared_hi"), sem("shared_split")
        down_done, result_made = sem("down_done"), sem("result_made")
        stored = [sem(f"stored{h}") for h in range(2)]

        block = ctx.enter_context(nc.Block())

        def wait(eng, semaphore, value):
            if not isinstance(value, int) or value > 0:
                eng.wait_ge(semaphore, value)

        def wait_alone(eng, semaphore, value):
            if not isinstance(value, int):
                value = eng.snap(eng.to_reg(value))
                eng.wait_ge(consts_made, 1)
            eng.wait_ge(semaphore, value)

        def sweep(eng, body, start, loops, stop, order=None, per=0):
            n = start
            for a, b in (*loops, (stop, stop)):
                for n in range(n, a):
                    body(n, n % 2, n)
                if b > a:
                    with eng.Fori(0, (b - a) // 2) as i:
                        if order:
                            order.loop(i, per, (b - a) // 2)
                        body(i * 2 + a, a % 2, a)
                        body(i * 2 + (a + 1), (a + 1) % 2, a + 1)
                        if order:
                            order.end()
                n = b

        NODES = (0, ((2, STEPS[0] - 2),), NB)
        DOUBLE = STEPS[1] - NB + 2
        FIRST = (0, ((2, DOUBLE), (DOUBLE, NB - 4)), NB)
        SECOND = (0, ((6, NB - 2),), NB + 3)

        def h_at(t, at):
            if at < INNER:
                return rows[:, bass.ds(t + OUTER, 1), :].rearrange("p o d -> p (o d)")
            return result[:, t - INNER, :].bitcast(F16)

        @block.sync
        def _(sp):
            sp.dma_start(src_i[:, :], src.rearrange("(p c) -> p c", p=P)).then_inc(s_src, 16)
            xv = x.rearrange("(b p) d -> p b d", p=P)
            for q, (a, b) in enumerate(PIECES):
                sp.dma_start(acc[:, a:b, :], xv[:, a:b, :]).then_inc(s_x[q], 16)
                if q == 2:
                    sp.dma_start(dst_i[:, :], dst.rearrange("(p c) -> p c", p=P)).then_inc(s_edge, 16)
                    sp.dma_start(w_in[:, :], w.rearrange("(p c) -> p c", p=P)).then_inc(s_edge, 16)
                    sp.dma_start(wg_in[:, :, :], wg.rearrange("(k p) f -> p k f", p=P)).then_inc(s_wg, 16)
            for k in range(KD):
                sp.dma_start(w1_in[:, k, :].rearrange("p (e f) -> p e f", e=NE),
                             w1[:, k * P:(k + 1) * P, :].rearrange("e p f -> p e f")).then_inc(s_w1, 16)
            sp.dma_start(w2_in[:, :, :], w2.rearrange("e f d -> (e f) d").rearrange("(k p) d -> p k d", p=P))\
              .then_inc(s_w2, 16)
            sp.dma_start(gw_in[:, :, :], gate_w.rearrange("(k p) e -> p k e", p=P)).then_inc(s_small, 16)
            sp.dma_start(gate_bias[:, :], gate_b.partition_broadcast(P)).then_inc(s_small, 16)
            sp.dma_start(b1_col[:, :], b1.rearrange("e f -> (e f)").rearrange("(k p) -> p k", p=P),
                         allow_slow_non_contiguous=True).then_inc(s_small, 16)
            sp.wait_ge(consts_made, 1)
            for row in range(0, STACK, 32):
                sp.dma_start(b2_in[row:row + NE, :], b2).then_inc(s_small, 16)

            def store_h(t, h, at):
                sp.wait_ge(h_split, t + 1)
                sp.dma_start(h_dram[bass.ds(t * P, P), :], h_at(t, at)).then_inc(h_stored, 16)
            sweep(sp, store_h, 0, ((0, INNER),), NB)

            def store(b, h, at):
                sp.wait_ge(result_made, b + 1)
                sp.dma_start(out[bass.ds(b * P, P), :], result[:, h, :]).then_inc(stored[h], 16)
            sweep(sp, store, 0, ((0, NB),), NB)
            for h in range(2):
                sp.wait_ge(stored[h], 16 * NB // 2)
            sp.wait_ge(h_stored, 16 * NB)

        @block.gpsimd
        def _(g):
            own = Order(g, pool, wait_alone)
            own(nc.gpsimd.memset(tri[:, :], 0.0))
            own(nc.gpsimd.affine_select(out=tri[:, :], in_=tri[:, :], compare_op=ALU.is_gt, fill=-1.0,
                                        base=0, pattern=[[1, P]], channel_multiplier=-1))
            own(nc.gpsimd.memset(ones[:, :], 1.0))
            own(nc.gpsimd.memset(keep, 1.0))
            for c in range(PARTS):
                own(nc.gpsimd.memset(keep.rearrange("p (s c) -> p s c", c=T)[:, :, C0[c]:C0[c] + 1], 0.0))
            for eye in (ident, ident16):
                own(nc.gpsimd.memset(eye[:, :], 0.0))
                own(nc.gpsimd.affine_select(out=eye[:, :], in_=eye[:, :], compare_op=ALU.not_equal, fill=1.0,
                                            base=0, pattern=[[-1, P]], channel_multiplier=1))
            own(nc.gpsimd.memset(b2_in[:, :], 0.0))
            own(nc.gpsimd.memset(at16[:, :, :, :], 0.0))
            nc.gpsimd.memset(share16[:, :, :, :], 0.0).then_inc(consts_made, 1)
            own(nc.gpsimd.iota(iota[:, :], pattern=[[1, P]], base=0, channel_multiplier=0,
                               allow_small_or_imprecise_dtypes=True))
            own(nc.gpsimd.iota(iota_t[:, :, :], pattern=[[1, QM], [0, TI]], base=0, channel_multiplier=0,
                               allow_small_or_imprecise_dtypes=True))
            own(nc.gpsimd.iota(iota8[:, :], pattern=[[1, NE]], base=0, channel_multiplier=0,
                               allow_small_or_imprecise_dtypes=True))
            own(nc.gpsimd.memset(expert_rows[:, :, :], 0.0))
            for row in (0, 64):
                part = expert_rows[row:row + NE, :, :].rearrange("e k (a f) -> e k a f", a=2)
                last = nc.gpsimd.affine_select(out=part, in_=part, compare_op=ALU.not_equal, fill=1.0, base=0,
                                               pattern=[[-2, KF], [-1, 2], [0, FF]], channel_multiplier=1)
                own(last)
            nc.gpsimd.memset(spill_at[:, :], 0).then_inc(consts_made, 1)

            def scaled(whole, hi):
                own(nc.gpsimd.tensor_scalar(whole, whole, SC_M, None, ALU.mult))
                own(nc.gpsimd.tensor_copy(hi, whole))

            def split(n, whole, hi, lo):
                scaled(whole, hi)
                nc.gpsimd.tensor_tensor(lo, whole, hi, ALU.subtract).then_inc(weights_split, 1)
                g.wait_ge(weights_split, n)

            g.wait_ge(s_w1, 16 * KD)
            split(1, w1_in[:, :, :], w1s[:, 0, :, :], w1s[:, 1, :, :])
            g.wait_ge(s_w2, 16)
            split(2, w2_in[:, :, :], w2s[:, 0, :, :], w2s[:, 1, :, :])
            g.wait_ge(s_small, 96)
            split(3, gw_in[:, :, :], gws[:, 0, :, :], gws[:, 1, :, :])
            scaled(b2_in[:, :], b2s[:, :])
            low = slice(32, 32 + NE)
            nc.gpsimd.tensor_tensor(b2s[low, :], b2_in[low, :], b2s[low, :], ALU.subtract).then_inc(weights_split, 1)
            g.wait_ge(weights_split, 4)

            g.wait_ge(h_stored, 16 * NB)

            def gather(n, h, at):
                c = at // NB
                wait_alone(g, staged, n + 1)
                for j in range(GT[c]):
                    g.indirect_dma_start(rows[:, SLOT0[c][h] + j, :], None, h_dram[:, :],
                                         bass.IndirectOffsetOnAxis(ap=at_i[:, h, j:j + 1], axis=0))\
                     .then_inc(gathered[h][j // TI], 16)
            sweep(g, gather, 0, ((0, NB),), NB)

            g.wait_ge(spill_known, 1)
            spill = g.value_load(spill_i[0:1, 0:1], min_val=0, max_val=E)
            with g.If(spill > 0):
                with g.Fori(0, T) as t:
                    g.wait_ge(sp_read, t * NB + 1)
                    nc.gpsimd.tensor_copy(spill_at[:, :], dst_i[:, bass.ds(t, 1)]).then_inc(sp_idx, 1)
                    wait_alone(g, sp_idx, t + 1)
                    g.indirect_dma_start(spill_rows[:, :], None, h_dram[:, :],
                                         bass.IndirectOffsetOnAxis(ap=spill_at[:, 0:1], axis=0)).then_inc(sp_got, 16)
            sweep(g, gather, NB, ((NB, 2 * NB),), 2 * NB)

        @block.scalar
        def _(a):
            own = Order(a, act, wait_alone)
            for q, (start, stop) in enumerate(PIECES[:-1]):
                a.wait_ge(s_x[q], 16)
                tiles = range(start, stop)
                for b in tiles:
                    last = nc.scalar.activation(xn[:, b % 2, :], acc[:, b, :], ACT.Copy, accum_out=sums[:, b:b + 1])
                    own(last)
                own(nc.scalar.activation(neg_mean[:, start:stop], sums[:, start:stop], ACT.Copy, scale=-1.0 / D))
                for b in tiles:
                    own(nc.scalar.activation(xn[:, b % 2, :], acc[:, b, :], ACT.Square, bias=neg_mean[:, b:b + 1],
                                             accum_out=squares[:, b:b + 1]))
            nc.scalar.activation(sums[:, 0:1], neg_mean[:, 0:1], ACT.Copy).then_inc(squares_made, 1)
            for k in range(KD):
                a.wait_ge(wgT_moved, k + 1)
                nc.scalar.activation(wgT[:, 0, k, :], bank[2 + k][:, :], ACT.Copy, scale=SC_M).then_inc(wgT_hi, 1)
            a.wait_ge(unfit_summed, 1)
            nc.scalar.activation(spill_i[:, :], bank[1][:, 0:1], ACT.Copy).then_inc(spill_known, 1)
            a.wait_ge(rstd_made, 1)

            def rows_of(t, h):
                wait(a, xnT_moved, t - 1)
                nc.scalar.activation(xn[:, h, :], acc[:, bass.ds(t, 1), :].rearrange("p o d -> p (o d)"),
                                     ACT.Identity, bias=shift[:, bass.ds(t, 1)], scale=rstd[:, bass.ds(t, 1)])\
                  .then_inc(xn_made, 1)

            def transposed_hi(t, h):
                a.wait_ge(xnT_moved, t + 1)
                wait(a, h_summed, t - 1)
                nc.scalar.activation(xnT[:, h, 0, :, :].rearrange("p k n -> p (k n)"), bank[X_BANK[h]][:, :],
                                     ACT.Copy, scale=SC_X).then_inc(xnT_hi, 1)

            def places_low(c, s, h):
                a.wait_ge(plain_made, s + (S0[c] + 1))
                for j in range(STEP):
                    last = nc.scalar.activation(rows_oh[h][:, 3, j // TI, :, j % TI], plain_oh[:, h, j // TI, :, j % TI],
                                                ACT.Copy, scale=w_low[:, bass.ds(s * STEP + (C0[c] + j), 1)])
                last.then_inc(low_made, 1)

            def copy_part(c):
                a.wait_ge(part_sorted, c + 1)
                for f in range(4):
                    nc.scalar.activation(sorted_f[:, f, Q0[c]:Q0[c] + Q[c]], bank[SORT_BANK[f]][:, 0:Q[c]], ACT.Copy)\
                      .then_inc(part_copied, 1)
                a.wait_ge(part_copied, 4 * (c + 1))

            def stage(n, h, at):
                c = at // NB
                first = bass.ds(n * GT[c] + (Q0[c] - c * NB * GT[c]), GT[c])
                wait(a, sums_done, n - 1)
                nc.scalar.activation(at16[:, h, :, 0:GT[c]], sorted_f[:, 1:4, first], ACT.Copy)
                nc.scalar.activation(at_i[:, h, 0:GT[c]], sorted_f[:, 0, first], ACT.Copy).then_inc(staged, 1)

            def node(t, h, at):
                if at < NB - 1:
                    transposed_hi(t + 1, 1 - h)
                if at < NB - 2:
                    rows_of(t + 2, h)
                if at < STEPS[0] - 1:
                    places_low(0, t + 1, 1 - h)
                elif at == NB - 3:
                    copy_part(0)
                    stage(0, 0, 0)
                    stage(1, 1, 1)
                elif at == NB - 1:
                    places_low(1, 0, 0)
                a.wait_ge(h_summed, t + 1)
                nc.scalar.activation(h_at(t, at)[:, 0:D], bank[H_BANK[h]][:, :],
                                     ACT.Copy, scale=SC_H / (SC_X * SC_M)).then_inc(h_hi, 1)
            rows_of(0, 0)
            rows_of(1, 1)
            transposed_hi(0, 0)
            places_low(0, 0, 0)
            sweep(a, node, *NODES)

            def times_ratio(n, h, sub):
                arrived = (n - (h + NB)) * (8 * TI) + (16 * TI + 8 * NB * SUB[0][sub])
                a.wait_ge(gathered[h][sub], arrived)
                wait(a, folded, (n - NB) * FOLDED + (sub - 1))
                for t in range(TI):
                    last = nc.scalar.activation(ratio_rows[:, sub, t, :], rows[:, SLOT0[1][h] + sub * TI + t, 0:D],
                                                ACT.Copy, scale=ratio[:, bass.ds((n - NB) * GT[1] + (sub * TI + t), 1)])
                last.then_inc(ratio_rows_made, 1)


            def first_sweep(n, h, at):
                if at < DOUBLE:
                    places_low(1, n * 2 + 2, 0)
                    places_low(1, n * 2 + 3, 1)
                elif at < NB - 4:
                    places_low(1, n + (DOUBLE + 2), h)
                elif at == NB - 2:
                    copy_part(1)
                stage(n + 2, h, at + 2)
            places_low(1, 1, 1)
            sweep(a, first_sweep, *FIRST)

            a.wait_ge(s_small, 96)
            a.wait_ge(ratio_made, 1)
            for sub in range(FOLDED):
                times_ratio(NB, 0, sub)

            def second_sweep(p, h, at):
                b, d, bh = p - 1, p - 2, 1 - h
                row = acc[:, bass.ds(p, 1), :].rearrange("p o d -> p (o d)") if at < NB else None
                if 2 <= at < NB + 2:
                    a.wait_ge(shareT_moved, d + 1)
                    nc.scalar.activation(shareT[:, h, :], bank[SHARE_T][0:STACK, 0:P // 2].bitcast(F16), ACT.Copy)\
                      .then_inc(shareT_made, 1)
                if at < NB - 1:
                    times_ratio(p + (NB + 1), bh, 0)
                if 1 <= at < NB + 1:
                    a.wait_ge(yT_moved, b + 1)
                    nc.scalar.activation(xnT[:, bh, 0, :, :].rearrange("p k n -> p (k n)"), bank[XT2][:, :],
                                         ACT.Copy, scale=SC_X).then_inc(yT_hi, 1)
                if 2 <= at < NB + 2:
                    a.wait_ge(shared_made, d + 1)
                    nc.scalar.activation(sharedT[:, h, 0, :, :].rearrange("p k n -> p (k n)"), shared[:, h, :],
                                         ACT.Copy).then_inc(shared_hi, 1)
                if at < NB - 2:
                    stage(p + (NB + 2), h, NB)
                if at < NB:
                    wait_alone(a, mean_known, p + 1)
                    nc.scalar.activation(xn[:, h, :], row, ACT.Square, bias=neg_mean[:, h:h + 1],
                                         accum_out=squares[:, h:h + 1]).then_inc(squares2_made, 1)
                if 1 <= at < NB + 1:
                    a.wait_ge(top_known, b + 1)
                    nc.scalar.activation(tanh_half[:, bh, :], lead[:, bh, :], ACT.Tanh, scale=0.5).then_inc(tanh_done, 1)
                if at < NB - 1:
                    times_ratio(p + (NB + 1), bh, 1)
                if at < NB:
                    wait_alone(a, shift_known, p + 1)
                    nc.scalar.activation(xn[:, h, :], row, ACT.Identity, bias=shift[:, h:h + 1],
                                         scale=rstd[:, h:h + 1]).then_inc(y_made, 1)
                if 1 <= at < NB + 1:
                    a.wait_ge(up_done, b + 1)
                    for k in range(KF):
                        last = nc.scalar.activation(hidden[:, bh, k * P:(k + 1) * P], bank[UP][:, k * P:(k + 1) * P],
                                                    ACT.Gelu, bias=b1_col[:, k:k + 1], scale=1.0 / (SC_X * SC_M))
                    last.then_inc(hidden_made, 1)
            sweep(a, second_sweep, *SECOND)

        @block.vector
        def _(v):
            own = Order(v, vec, wait_alone)

            def rsqrt_newton(y, xv, t):
                nc.vector.tensor_scalar(y.bitcast(I32), xv.bitcast(I32), -0.5, MAGIC, ALU.mult, ALU.add)
                own(nc.vector.tensor_scalar(xv, xv, -0.5, None, ALU.mult))
                for _ in range(3):
                    if y.shape[-1] == 1:
                        own(nc.vector.scalar_tensor_tensor(t, y, y, xv, ALU.mult, ALU.mult))
                    else:
                        own(nc.vector.tensor_tensor(t, y, y, ALU.mult))
                        own(nc.vector.tensor_tensor(t, t, xv, ALU.mult))
                    own(nc.vector.scalar_tensor_tensor(y, t, 1.5, y, ALU.add, ALU.mult))

            v.wait_ge(s_src, 16)
            own(nc.vector.tensor_scalar(block_i[:, :], src_i[:, :], 7, None, ALU.logical_shift_right))
            own(nc.vector.tensor_copy(block16[:, :], block_i[:, :]))
            v.wait_ge(consts_made, 1)
            for b in range(NB):
                last = nc.vector.tensor_scalar(onehot[:, b, :], block16[:, :], float(b), None, ALU.is_equal)
            own(last)
            for r in range(NB // RB):
                some = slice(r * RB, (r + 1) * RB)
                nc.vector.tensor_tensor_scan(counted[:, some, :].rearrange("p b c -> p (b c)"), keep,
                                             onehot[:, some, :].rearrange("p b c -> p (b c)"),
                                             0.0, ALU.mult, ALU.add).then_inc(onehot_made, 1)
            nc.vector.tensor_scalar(local_i[:, :], src_i[:, :], P - 1, None, ALU.bitwise_and)
            part = [slice(C0[c], C0[c] + CT[c]) for c in range(PARTS)]
            for c in range(PARTS):
                last = nc.vector.tensor_scalar(first_tile[:, part[c]], block16[:, part[c]], float(GT[c]), None, ALU.mult)
            own(last)
            v.wait_ge(s_edge, 32)
            nc.vector.tensor_copy(field[:, 1, :], local_i[:, :])
            nc.vector.tensor_copy(field[:, 0, :], dst_i[:, :])
            own(nc.vector.tensor_scalar(field[:, 2, :], w_in[:, :], SC_W, None, ALU.mult))
            own(nc.vector.scalar_tensor_tensor(field[:, 3, :], w_in[:, :], SC_W, field[:, 2, :],
                                               ALU.mult, ALU.subtract))
            nc.vector.tensor_copy(w_low[:, :], field[:, 3, :]).then_inc(w_low_made, 1)
            for r in range(NB // RB):
                v.wait_ge(counts_summed, r + 1)
                for q in range(2):
                    two = slice(r * RB + 2 * q, r * RB + 2 * q + 2)
                    last = nc.vector.scalar_tensor_tensor(
                        picked[:, two, :].rearrange("p b c -> p (b c)"), bank[2 * r + q][:, :], 2047.0,
                        onehot[:, two, :].rearrange("p b c -> p (b c)"), ALU.min, ALU.mult)
                last.then_inc(picked_made, 1)
            v.wait_ge(ranks_summed, 1)
            rank = bank[0][:, 0:T]
            for c in range(PARTS):
                nc.vector.tensor_scalar(unfit[:, part[c]], bank[0][:, part[c]], float(cap[c]), 0.0, ALU.is_ge, ALU.add,
                                        accum_out=unfit_sum[:, c:c + 1])
            own(nc.vector.tensor_copy(rank_i[:, :], rank))
            own(nc.vector.tensor_scalar(slot_i[:, 1, :], rank_i[:, :], 7, None, ALU.logical_shift_right))
            nc.vector.tensor_tensor(unfit16[:, :], unfit_sum[:, 0:1], unfit_sum[:, 1:2], ALU.add).then_inc(unfit_made, 1)
            own(nc.vector.tensor_scalar(slot_i[:, 0, :], rank_i[:, :], P - 1, None, ALU.bitwise_and))
            own(nc.vector.tensor_tensor(first_tile[:, :], first_tile[:, :], slot_i[:, 1, :], ALU.add))
            nc.vector.tensor_copy(slot[:, 0, :], slot_i[:, 0, :])
            own(nc.vector.scalar_tensor_tensor(slot[:, 1, :], unfit[:, :], 4096.0, first_tile[:, :],
                                               ALU.mult, ALU.add))

            v.wait_ge(s_x[-1], 16)
            done = PIECES[-1][0]
            for b in range(done, NB):
                last = nc.vector.bn_stats(stats[:, b - done, :], acc[:, b, :])
            own(last)
            for b in range(done, NB):
                last = nc.vector.bn_aggr(mv[:, b - done, :], stats[:, b - done, :])
            own(last)
            nc.vector.tensor_scalar(neg_mean[:, done:], mv[:, 0:NB - done, 0], -1.0, None, ALU.mult)
            nc.vector.tensor_scalar(var[:, done:], mv[:, 0:NB - done, 1], EPS, None, ALU.add)
            v.wait_ge(squares_made, 1)
            own(nc.vector.tensor_scalar(var[:, :done], squares[:, :done], 1.0 / D, EPS, ALU.mult, ALU.add))
            rsqrt_newton(rstd[:, :], var[:, :], newton[:, :])
            nc.vector.tensor_tensor(shift[:, :], neg_mean[:, :], rstd[:, :], ALU.mult).then_inc(rstd_made, 1)
            for k in range(KD):
                v.wait_ge(wgT_hi, k + 1)
                nc.vector.scalar_tensor_tensor(wgT[:, 1, k, :], bank[2 + k][:, :], SC_M, wgT[:, 0, k, :],
                                               ALU.mult, ALU.subtract).then_inc(wgT_split, 1)
            v.wait_ge(consts_made, 2)

            def transposed_low(t, h):
                v.wait_ge(xnT_hi, t + 1)
                nc.vector.scalar_tensor_tensor(xnT[:, h, 1, :, :].rearrange("p k n -> p (k n)"), bank[X_BANK[h]][:, :],
                                               SC_X, xnT[:, h, 0, :, :].rearrange("p k n -> p (k n)"),
                                               ALU.mult, ALU.subtract).then_inc(xnT_split, 1)

            def h_low(t, h, at):
                v.wait_ge(h_hi, t + 1)
                nc.vector.scalar_tensor_tensor(h_at(t, at)[:, D:2 * D], bank[H_BANK[h]][:, :], SC_H / (SC_X * SC_M),
                                               h_at(t, at)[:, 0:D], ALU.mult, ALU.subtract).then_inc(h_split, 1)

            def spread(tiles, groups, ti, width):
                return tiles.rearrange("p (g t) -> p g t", t=ti).unsqueeze(2).to_broadcast([P, groups, width, ti])

            def repeated(table, groups, width, ti):
                return table[:, 0:width, :].unsqueeze(1).to_broadcast([P, groups, width, ti])

            def places_plain(c, s, h):
                wait(v, places_used, s + (S0[c] - 1))
                G = STEP // TI
                at = bass.ds(s * STEP + C0[c], STEP)
                nc.vector.tensor_tensor(plain_oh[:, h], repeated(iota_t, G, P, TI), spread(slot[:, 0, at], G, TI, P),
                                        ALU.is_equal).then_inc(plain_made, 1)

            def places(c, s, h):
                G = STEP // TI
                at = bass.ds(s * STEP + C0[c], STEP)
                nc.vector.tensor_tensor(tile_oh[:, h, :, 0:Q[c], :], repeated(iota_t, G, Q[c], TI),
                                        spread(slot[:, 1, at], G, TI, Q[c]), ALU.is_equal)
                v.wait_ge(plain_made, s + (S0[c] + 1))
                for f in range(3):
                    last = nc.vector.tensor_tensor(rows_oh[h][:, f], plain_oh[:, h], spread(field[:, f, at], G, TI, P),
                                                   ALU.mult)
                last.then_inc(places_made, 1)

            def node(t, h, at):
                if at < STEPS[0] - 1:
                    places_plain(0, t + 1, 1 - h)
                if at < NB - 1:
                    transposed_low(t + 1, 1 - h)
                if at > 0:
                    h_low(t - 1, 1 - h, at - 1)
                if at < STEPS[0] - 1:
                    places(0, t + 1, 1 - h)
                elif at == NB - 2:
                    places_plain(1, 0, 0)
                elif at == NB - 1:
                    places(1, 0, 0)
            places_plain(0, 0, 0)
            transposed_low(0, 0)
            places(0, 0, 0)
            sweep(v, node, *NODES)
            h_low(NB - 1, 1, NB - 1)

            def select_plain(n, h, at):
                v.wait_ge(staged, n + 1)
                wait(v, wsel_made, n)
                G = SUBS[at // NB]
                nc.vector.tensor_tensor(plain_sel[:, 0:G, :, :], repeated(iota_t, G, P, TI),
                                        spread(at16[:, h, 0, 0:G * TI], G, TI, P), ALU.is_equal)\
                  .then_inc(sel_made, 1)

            def select(n, h, at, half):
                G = SUBS[at // NB]
                first = FOLDED * (half * (at // NB))
                v.wait_ge(sel_made, n + 1)
                nc.vector.tensor_tensor(wsel[:, h, half, first:G], plain_sel[:, first:G, :, :],
                                        spread(at16[:, h, 1 + half, first * TI:G * TI], G - first, TI, P),
                                        ALU.mult).then_inc((high_made, wsel_made)[half], 1)

            def select_all(n, h, at):
                select_plain(n, h, at)
                select(n, h, at, 0)
                select(n, h, at, 1)

            def fold(n, h, sub):
                v.wait_ge(ratio_rows_made, (n - NB) * FOLDED + (sub + 1))
                low = rows[:, SLOT0[1][h] + sub * TI:SLOT0[1][h] + (sub + 1) * TI, D:2 * D]
                nc.vector.tensor_tensor(low, low, ratio_rows[:, sub, :, :], ALU.add).then_inc(folded, 1)

            def add_messages(n, b, h):
                v.wait_ge(sums_done, n + 1)
                row = acc[:, bass.ds(b, 1), :].rearrange("p o d -> p (o d)")
                nc.vector.scalar_tensor_tensor(row, bank[SUM_BANK[h]][:, :], 1.0 / (SC_W * SC_H), row,
                                               ALU.mult, ALU.add).then_inc(sums_read, 1)

            def places_all(s, h):
                places_plain(1, s, h)
                places(1, s, h)
            places_all(1, 1)
            select_all(0, 0, 0)

            def first_sweep(n, h, at):
                if at == 0:
                    places_all(2, 0)
                select_all(n + 1, 1 - h, at + 1)
                if at == 0:
                    places_all(3, 1)
                elif at < DOUBLE:
                    places_all(n * 2 + 2, 0)
                    places_all(n * 2 + 3, 1)
                elif at < NB - 4:
                    places_all(n + (DOUBLE + 2), h)
                add_messages(n, n, h)
            sweep(v, first_sweep, *FIRST)
            v.wait_ge(sums_read, NB)
            v.wait_ge(part_copied, 4 * PARTS)
            own(nc.vector.tensor_scalar(ratio_den[:, :], sorted_f[:, 2, Q0[1]:], 0.0, None, ALU.is_equal))
            own(nc.vector.tensor_tensor(ratio_den[:, :], ratio_den[:, :], sorted_f[:, 2, Q0[1]:], ALU.add))
            own(nc.vector.reciprocal(ratio_den[:, :], ratio_den[:, :]))
            nc.vector.tensor_tensor(ratio[:, :], ratio_den[:, :], sorted_f[:, 3, Q0[1]:], ALU.mult).then_inc(ratio_made, 1)

            v.wait_ge(spill_known, 1)
            spill = v.value_load(spill_i[0:1, 0:1], min_val=0, max_val=E)
            with v.If(spill > 0):
                for half in range(2):
                    nc.vector.tensor_tensor(spill_w[:, half, :], field[:, 2 + half, :], unfit[:, :], ALU.mult)\
                      .then_inc((sp_read, sp_sel)[half], 1)
                with v.Fori(0, T) as t:
                    v.wait_ge(sp_sel, t * (2 * NB + 1) + 1)
                    nc.vector.tensor_copy(spill_src[:, :], src_i[:, bass.ds(t, 1)]).then_inc(sp_sel, 1)
                    with v.Fori(0, NB) as b:
                        turn = t * NB + b
                        v.wait_ge(sp_sel, turn * 2 + t + 2)
                        for half in range(2):
                            last = nc.vector.tensor_scalar(spill_sel[:, half, :], iota[:, :], spill_src[:, 0:1],
                                                           spill_w[:, half, bass.ds(t, 1)], ALU.is_equal, ALU.mult)
                        last.then_inc(sp_sel, 1)
                        v.wait_ge(sp_sel, turn * 2 + t + 3)
                        nc.vector.tensor_scalar(spill_src[:, :], spill_src[:, :], -float(P), None, ALU.add)\
                          .then_inc(sp_sel, 1)
                        v.wait_ge(sp_sum, turn + 1)
                        row = acc[:, bass.ds(b, 1), :].rearrange("p o d -> p (o d)")
                        nc.vector.scalar_tensor_tensor(row, bank[GATE][:, :], 1.0 / (SC_W * SC_H), row,
                                                       ALU.mult, ALU.add).then_inc(sp_read, 1)
                v.wait_ge(sp_read, T * NB + 1)

            for sub in range(FOLDED):
                fold(NB, 0, sub)
            def finish(p, bh, at):
                v.wait_ge(down_done, p - 2)
                if at >= 5:
                    v.wait_ge(stored[bh], (p - (3 + bh)) * 8)
                nc.vector.scalar_tensor_tensor(result[:, bh, :], bank[DOWN][:, :], 1.0 / (SC_C * SC_M),
                                               acc[:, bass.ds(p - 3, 1), :].rearrange("p o d -> p (o d)"),
                                               ALU.mult, ALU.add).then_inc(result_made, 1)

            def second_sweep(p, h, at):
                b, d, bh = p - 1, p - 2, 1 - h
                row = acc[:, bass.ds(p, 1), :].rearrange("p o d -> p (o d)") if at < NB else None
                if 3 <= at and at != NB + 1:
                    finish(p, bh, at)
                if at < NB - 1:
                    select_all(p + (NB + 1), bh, NB)
                if 2 <= at < NB + 2:
                    v.wait_ge(hidden_made, d + 1)
                    v.wait_ge(spread_done, d + 1)
                    nc.vector.tensor_tensor(shared[:, h, :], hidden[:, h, :], bank[SHARE][:, :], ALU.mult)\
                      .then_inc(shared_made, 1)
                if 1 <= at < NB + 1:
                    v.wait_ge(yT_hi, b + 1)
                    nc.vector.scalar_tensor_tensor(xnT[:, bh, 1, :, :].rearrange("p k n -> p (k n)"), bank[XT2][:, :],
                                                   SC_X, xnT[:, bh, 0, :, :].rearrange("p k n -> p (k n)"),
                                                   ALU.mult, ALU.subtract).then_inc(yT_split, 1)
                if at < NB - 1:
                    fold(p + (NB + 1), bh, 0)
                if at < NB:
                    v.wait_ge(sums_done, p + (NB + 1))
                    nc.vector.scalar_tensor_tensor(row, bank[SUM_BANK[h]][:, :], 1.0 / (SC_W * SC_H), row,
                                                   ALU.mult, ALU.add, accum_out=sums[:, h:h + 1]).then_inc(sums_read, 1)
                    v.wait_ge(sums_read, p + (NB + 1))
                    nc.vector.tensor_scalar(neg_mean[:, h:h + 1], sums[:, h:h + 1], -1.0 / D, None, ALU.mult)\
                      .then_inc(mean_known, 1)
                if 1 <= at < NB + 1:
                    v.wait_ge(gate_done, b + 1)
                    own(nc.vector.scalar_tensor_tensor(logits[:, bh, :], bank[GATE][:, 0:NE], 1.0 / (SC_X * SC_M),
                                                       gate_bias[:, :], ALU.mult, ALU.add), alone=True)
                    own(nc.vector.max(top[:, bh, :], logits[:, bh, :]))
                    nc.vector.tensor_tensor(lead[:, bh, :], top[:, bh, 0:1], top[:, bh, 1:2], ALU.subtract)\
                      .then_inc(top_known, 1)
                    own(nc.vector.max_index(top_at[:, bh, :], top[:, bh, :], logits[:, bh, :]))
                    nc.vector.tensor_copy(top_f[:, bh, :], top_at[:, bh, 0:2])
                if 2 <= at < NB + 2:
                    v.wait_ge(shared_hi, d + 1)
                    nc.vector.tensor_tensor(sharedT[:, h, 1, :, :].rearrange("p k n -> p (k n)"), shared[:, h, :],
                                            sharedT[:, h, 0, :, :].rearrange("p k n -> p (k n)"), ALU.subtract)\
                      .then_inc(shared_split, 1)
                if at == NB + 1:
                    finish(p, bh, at)
                if at < NB:
                    v.wait_ge(squares2_made, p + 1)
                    own(nc.vector.tensor_scalar(var[:, h:h + 1], squares[:, h:h + 1], 1.0 / D, EPS, ALU.mult, ALU.add))
                    rsqrt_newton(rstd[:, h:h + 1], var[:, h:h + 1], newton[:, h:h + 1])
                    nc.vector.tensor_tensor(shift[:, h:h + 1], neg_mean[:, h:h + 1], rstd[:, h:h + 1], ALU.mult)\
                      .then_inc(shift_known, 1)
                if 1 <= at < NB + 1:
                    v.wait_ge(tanh_done, b + 1)
                    nc.vector.tensor_scalar(top_share[:, bh, 0:1], tanh_half[:, bh, :], 0.5 * SC_C, 0.5 * SC_C,
                                            ALU.mult, ALU.add)
                    own(nc.vector.tensor_scalar(top_share[:, bh, 1:2], tanh_half[:, bh, :], -0.5 * SC_C, 0.5 * SC_C,
                                                ALU.mult, ALU.add))
                    nc.vector.tensor_scalar(share[:, bh, :], iota8[:, :], top_f[:, bh, 0:1], top_share[:, bh, 0:1],
                                            ALU.is_equal, ALU.mult)
                    own(nc.vector.tensor_scalar(second_share[:, bh, :], iota8[:, :], top_f[:, bh, 1:2],
                                                top_share[:, bh, 1:2], ALU.is_equal, ALU.mult))
                    own(nc.vector.tensor_tensor(share[:, bh, :], share[:, bh, :], second_share[:, bh, :], ALU.add))
                    own(nc.vector.tensor_copy(share16[:, bh, 0:2, 0:NE],
                                              share[:, bh, :].unsqueeze(1).to_broadcast([P, 2, NE])))
                    nc.vector.tensor_tensor(share16[:, bh, 2, 0:NE], share[:, bh, :], share16[:, bh, 0, 0:NE],
                                            ALU.subtract).then_inc(share_made, 1)
                if at < NB - 1:
                    fold(p + (NB + 1), bh, 1)
            sweep(v, second_sweep, *SECOND, order=own, per=2 * (3 + 8 + 4))

        @block.tensor
        def _(pe):
            def split_product(out_ap, pairs, more=()):
                terms = [t for (lh, ll), (rh, rl) in pairs for t in ((lh, rh), (lh, rl), (ll, rh))] + list(more)
                for n, (left, right) in enumerate(terms):
                    last = nc.tensor.matmul(out_ap, left, right, start=(n == 0), stop=(n == len(terms) - 1))
                return last

            pe.wait_ge(consts_made, 1)
            for r in range(NB // RB):
                pe.wait_ge(onehot_made, r + 1)
                for q in range(2):
                    two = slice(r * RB + 2 * q, r * RB + 2 * q + 2)
                    nc.tensor.matmul(bank[2 * r + q][:, :], ones[:, :],
                                     counted[:, two, :].rearrange("p b c -> p (b c)"), start=True, stop=False)
                    last = nc.tensor.matmul(bank[2 * r + q][:, :], tri[:, :],
                                            onehot[:, two, :].rearrange("p b c -> p (b c)"), start=False, stop=True)
                last.then_inc(counts_summed, 1)
            for r in range(NB // RB):
                pe.wait_ge(picked_made, r + 1)
                for b in range(r * RB, (r + 1) * RB):
                    last = nc.tensor.matmul(bank[0][:, 0:T], ident16[:, :], picked[:, b, :],
                                            start=(b == 0), stop=(b == NB - 1))
            last.then_inc(ranks_summed, 1)
            pe.wait_ge(s_wg, 16)
            for k in range(KD):
                for e in range(KD):
                    last = nc.tensor.transpose(bank[2 + k][:, e * P:(e + 1) * P], wg_in[:, e, k * P:(k + 1) * P],
                                               ident[:, :])
                last.then_inc(wgT_moved, 1)
            pe.wait_ge(unfit_made, 1)
            nc.tensor.matmul(bank[1][:, 0:1], ones[:, :], unfit16[:, :], start=True, stop=True)\
                .then_inc(unfit_summed, 1)

            def transpose_node(t, h):
                pe.wait_ge(xn_made, t + 1)
                wait(pe, xnT_split, t - 1)
                for k in range(KD):
                    last = nc.tensor.transpose(bank[X_BANK[h]][:, k * P:(k + 1) * P], xn[:, h, k * P:(k + 1) * P],
                                               ident[:, :])
                last.then_inc(xnT_moved, 1)

            def move(c, s, h, start=False, stop=False):
                pe.wait_ge(places_made, s + (S0[c] + 1))
                pe.wait_ge(low_made, s + (S0[c] + 1))
                for j in range(STEP):
                    for f in range(4):
                        last = nc.tensor.matmul(bank[SORT_BANK[f]][:, 0:Q[c]], rows_oh[h][:, f, j // TI, :, j % TI],
                                                tile_oh[:, h, j // TI, 0:Q[c], j % TI],
                                                start=start and j == 0, stop=stop and j == STEP - 1)
                last.then_inc(places_used, 1)
                if stop:
                    pe.wait_ge(xnT_split, NB if c else STEPS[0])
                    nc.tensor.matmul(bank[7][:, 0:P], ones[:, :], ones[:, :], start=True, stop=True)\
                        .then_inc(part_sorted, 1)

            def node(t, h, at):
                if at < NB - 1:
                    transpose_node(t + 1, 1 - h)
                pe.wait_ge(xnT_split, t + 1)
                wait(pe, h_split, t - 1)
                split_product(bank[H_BANK[h]][:, :],
                              [((xnT[:, h, 0, k, :], xnT[:, h, 1, k, :]), (wgT[:, 0, k, :], wgT[:, 1, k, :]))
                               for k in range(KD)]).then_inc(h_summed, 1)
                if at < STEPS[0]:
                    move(0, t, h, start=at == 0, stop=at == STEPS[0] - 1)
            transpose_node(0, 0)
            pe.wait_ge(wgT_split, KD)
            sweep(pe, node, *NODES)

            def messages(n, h, at, sub):
                c = at // NB
                if sub == 0:
                    pe.wait_ge(wsel_made, n + 1)
                    wait(pe, sums_read, n - 1)
                before = 8 * NB * (SUB[0][sub] if sub < SUBS[0] else 0) if c else 0
                tiles = SUB[c][sub]
                pe.wait_ge(gathered[h][sub], (n - (h + c * NB)) * (8 * tiles) + (16 * tiles + before))
                products = ((0, 0), (0, 1), (1, 0))
                if c and sub < FOLDED:
                    products = products[:2]
                    pe.wait_ge(folded, (n - NB) * FOLDED + (sub + 1))
                for t in range(tiles):
                    for half, cols in products:
                        last = nc.tensor.matmul(bank[SUM_BANK[h]][:, :], wsel[:, h, half, sub, :, t],
                                                rows[:, SLOT0[c][h] + sub * TI + t, cols * D:(cols + 1) * D],
                                                start=(sub == 0 and t == 0 and half == 0 and cols == 0),
                                                stop=(sub == SUBS[c] - 1 and t == tiles - 1 and half == 1))
                if sub == SUBS[c] - 1:
                    last.then_inc(sums_done, 1)

            pe.wait_ge(part_copied, 4)

            def first_sweep(n, h, at):
                if at == 0:
                    move(1, 0, 0, start=True)
                    move(1, 1, 1)
                    move(1, 2, 0)
                    pe.wait_ge(h_split, NB)
                    messages(n, h, at, 0)
                    messages(n, h, at, 1)
                elif at == 1:
                    messages(n, h, at, 0)
                    move(1, 3, 1)
                    messages(n, h, at, 1)
                elif at < DOUBLE:
                    move(1, n * 2, 0)
                    messages(n, h, at, 0)
                    move(1, n * 2 + 1, 1)
                    messages(n, h, at, 1)
                else:
                    messages(n, h, at, 0)
                    if at < NB - 2:
                        move(1, n + DOUBLE, h, stop=at == NB - 3)
                    messages(n, h, at, 1)
            sweep(pe, first_sweep, *FIRST)

            pe.wait_ge(part_copied, 8)
            pe.wait_ge(spill_known, 1)
            spill = pe.value_load(spill_i[0:1, 0:1], min_val=0, max_val=E)
            with pe.If(spill > 0):
                with pe.Fori(0, T) as t:
                    wait_alone(pe, sp_got, t * 16 + 16)
                    with pe.Fori(0, NB) as b:
                        turn = t * NB + b
                        pe.wait_ge(sp_sel, turn * 2 + t + 3)
                        pe.wait_ge(sp_read, turn + 1)
                        split_product(bank[GATE][:, :], [((spill_sel[:, 0, :], spill_sel[:, 1, :]),
                                                          (spill_rows[:, 0:D], spill_rows[:, D:2 * D]))])\
                            .then_inc(sp_sum, 1)
            pe.wait_ge(weights_split, 4)

            def transpose_shares(d, h):
                pe.wait_ge(share_made, d + 1)
                wait(pe, shareT_made, d)
                nc.tensor.transpose(bank[SHARE_T][0:STACK, 0:P // 2].bitcast(F16),
                                    share16[:, h].rearrange("p s e -> p (s e)"), ident16[:, :])\
                    .then_inc(shareT_moved, 1)

            def spread_shares(d, h):
                pe.wait_ge(shareT_made, d + 1)
                wait(pe, shared_made, d)
                for k in range(KF):
                    last = nc.tensor.matmul(bank[SHARE][:, k * P:(k + 1) * P], expert_rows[:, k, :],
                                            shareT[:, h, :], start=True, stop=True)
                last.then_inc(spread_done, 1)

            def second_sweep(p, h, at):
                b, d, bh = p - 1, p - 2, 1 - h
                if at < NB:
                    messages(p + NB, h, NB, 0)
                if 2 <= at < NB + 1:
                    transpose_shares(d, h)
                if at < NB:
                    messages(p + NB, h, NB, 1)
                if 2 <= at < NB + 1:
                    spread_shares(d, h)
                if 1 <= at < NB + 1:
                    pe.wait_ge(y_made, b + 1)
                    wait(pe, yT_split, b)
                    for k in range(KD):
                        last = nc.tensor.transpose(bank[XT2][:, k * P:(k + 1) * P], xn[:, bh, k * P:(k + 1) * P],
                                                   ident[:, :])
                    last.then_inc(yT_moved, 1)
                if at < NB:
                    messages(p + NB, h, NB, 2)
                if 1 <= at < NB + 1:
                    pe.wait_ge(yT_split, b + 1)
                    halves_of = [(xnT[:, bh, 0, k, :], xnT[:, bh, 1, k, :]) for k in range(KD)]
                    split_product(bank[GATE][:, 0:NE], [(halves_of[k], (gws[:, 0, k, :], gws[:, 1, k, :]))
                                                        for k in range(KD)]).then_inc(gate_done, 1)
                    wait(pe, hidden_made, b)
                    for f in range(KF):
                        cols = slice(f * P, (f + 1) * P)
                        last = split_product(bank[UP][:, cols], [((w1s[:, 0, k, cols], w1s[:, 1, k, cols]), halves_of[k])
                                                                 for k in range(KD)])
                    last.then_inc(up_done, 1)
                if at == NB:
                    transpose_shares(b, bh)
                    spread_shares(b, bh)
                if 2 <= at < NB + 2:
                    pe.wait_ge(shared_split, d + 1)
                    wait(pe, result_made, d)
                    split_product(bank[DOWN][:, :],
                                  [((sharedT[:, h, 0, k, :], sharedT[:, h, 1, k, :]),
                                    (w2s[:, 0, k, :], w2s[:, 1, k, :])) for k in range(KF)],
                                  more=[(shareT[:, h, :], b2s[:, :])]).then_inc(down_done, 1)
            sweep(pe, second_sweep, *SECOND)


_INS = ['x', 'src', 'dst', 'edge_weight', 'L0_gnn_weight', 'L0_ffn_Wg', 'L0_ffn_bg', 'L0_ffn_W1', 'L0_ffn_b1',
        'L0_ffn_W2', 'L0_ffn_b2']


def kernel(**inputs):
    import numpy as _np
    import concourse.bacc as _bacc
    from concourse import mybir as _mybir
    from concourse.bass_utils import run_bass_kernel_spmd as _run

    nc = _bacc.Bacc("TRN2", target_bir_lowering=False, num_devices=1)
    arrays, args = {}, []
    for name in _INS:
        a = _np.ascontiguousarray(inputs[name])
        arrays[f"in_{name}_dram"] = a
        args.append(nc.dram_tensor(f"in_{name}_dram", a.shape, _mybir.dt.from_np(a.dtype), kind="ExternalInput").ap())
    out = nc.dram_tensor("out_dram", (N, D), _mybir.dt.float32, kind="ExternalOutput").ap()
    h_dram = nc.dram_tensor("h_dram", (N, 2 * D), _mybir.dt.float16, kind="Internal").ap()
    gnn_moe(nc, *args, out, h_dram)
    r = _run(nc, [arrays], core_ids=[0])
    return r.results[0]["out_dram"]
```
